# Optimizing a Trainium2 kernel written in Bass

```python
import numpy as np
import jax
import jax.numpy as jnp

def _softmax(x, axis=-1):
    return jax.nn.softmax(x, axis=axis)

def _gelu(x):
    return jax.nn.gelu(x, approximate=True)

def _silu(x):
    return jax.nn.silu(x)

def _sigmoid(x):
    return jax.nn.sigmoid(x)

def _layernorm(x, axis=-1, eps=1e-05):
    m = jnp.mean(x, axis=axis, keepdims=True)
    v = jnp.var(x, axis=axis, keepdims=True)
    return (x - m) / jnp.sqrt(v + eps)

def _scatter_add(tgt, idx, src, axis=0):
    return tgt.at[idx].add(src)

def _segment_sum(src, seg, n):
    return jax.ops.segment_sum(src, seg, n)
kernel_name = 'mk_flamingo_gated_d1_seqx_r2_437b8b'

def setup_inputs(seed: int=0):
    np.random.seed(seed)
    _w = jnp.asarray

    def _rec_inputs():
        import jax
        import jax.numpy as jnp
        _rk = jax.random.key(seed)
        x = 7.22e-05 + 1 * jax.random.normal(jax.random.fold_in(_rk, 1), (8, 1024, 512), jnp.float32)
        _lenS = 1024 - jax.random.randint(jax.random.fold_in(_rk, 7), (8,), 0, max(1, 1024 // 4) + 1, jnp.int32)
        _lenS2 = 1024 - jax.random.randint(jax.random.fold_in(_rk, 8), (8,), 0, max(1, 1024 // 4) + 1, jnp.int32)
        _ctx_768P = jax.random.normal(jax.random.fold_in(_rk, 11), (8, 16, 384), jnp.float32)
        _ctx_768c = jax.random.dirichlet(jax.random.fold_in(_rk, 511), 0.3 * jnp.ones((16,), jnp.float32), (8, 1024))
        _ctx_768t = jnp.einsum('bsk,bkd->bsd', _ctx_768c, _ctx_768P)
        _ctx_768t = _ctx_768t * jax.lax.rsqrt(jnp.mean(jnp.square(_ctx_768t)) + 1e-12) * 0.953939
        ctx_768 = -0.000191848 + 0.999787 * (_ctx_768t + 0.3 * jax.random.normal(jax.random.fold_in(_rk, 611), (8, 1024, 384), jnp.float32))
        _g = jax.random.normal(jax.random.fold_in(_rk, 9001), (2, 1), jnp.float32)
        _g = jnp.sign(_g) * jnp.maximum(jnp.abs(_g), 1.0) + (_g == 0) * 1.0
        g_xattn = _g[0]
        g_ffn = _g[1]
        return (x, ctx_768, g_xattn, g_ffn)
    x, ctx_768, g_xattn, g_ffn = _rec_inputs()

    def _L0_xattn_setup():
        import jax, jax.numpy as jnp
        import numpy as np
        HEADS = 8
        DIM_HEAD = 64
        SCALE = DIM_HEAD ** (-0.5)
        key = jax.random.key(seed)
        ks = jax.random.split(key, 7)
        B, Nq, Nc = (4, 1024, 1024)
        Dq, Dc = (512, 384)
        inner = HEADS * DIM_HEAD
        x = jax.random.normal(ks[0], (B, Nq, Dq), dtype=jnp.float32)
        context = jax.random.normal(ks[1], (B, Nc, Dc), dtype=jnp.float32)
        Wq = jax.random.normal(ks[2], (Dq, inner), dtype=jnp.float32) * Dq ** (-0.5)
        Wk = jax.random.normal(ks[3], (Dc, inner), dtype=jnp.float32) * Dc ** (-0.5)
        Wv = jax.random.normal(ks[4], (Dc, inner), dtype=jnp.float32) * Dc ** (-0.5)
        Wo = jax.random.normal(ks[5], (inner, Dq), dtype=jnp.float32) * inner ** (-0.5)
        bo = jax.random.normal(ks[6], (Dq,), dtype=jnp.float32) * 0.01
        return {'x': x, 'context': context, 'Wq': Wq, 'Wk': Wk, 'Wv': Wv, 'Wo': Wo, 'bo': bo}
    _L0_xattn_all = _L0_xattn_setup()
    _L0_xattn_in = {k: v for k, v in _L0_xattn_all.items() if k in ('Wq', 'Wk', 'Wv', 'Wo', 'bo')}
    del _L0_xattn_all

    def _L0_ffn_setup():
        import jax, jax.numpy as jnp
        import numpy as np
        import math
        DIM = 512
        NUM_HEADS = 16
        SHARED_HEADS = 1
        ROUTED_HEADS = 3
        HEAD_DIM = DIM // NUM_HEADS
        B, N = (2, 1024)
        key = jax.random.key(seed)
        ks = jax.random.split(key, 16)
        s = 1.0 / math.sqrt(DIM)
        inp = {'x': jax.random.normal(ks[0], (B, N, DIM), dtype=jnp.float32), 'Wq': jax.random.uniform(ks[1], (DIM, DIM), minval=-s, maxval=s), 'bq': jax.random.uniform(ks[2], (DIM,), minval=-s, maxval=s), 'Wk': jax.random.uniform(ks[3], (DIM, DIM), minval=-s, maxval=s), 'bk': jax.random.uniform(ks[4], (DIM,), minval=-s, maxval=s), 'Wv': jax.random.uniform(ks[5], (DIM, DIM), minval=-s, maxval=s), 'bv': jax.random.uniform(ks[6], (DIM,), minval=-s, maxval=s), 'Wp': jax.random.uniform(ks[7], (DIM, DIM), minval=-s, maxval=s), 'bp': jax.random.uniform(ks[8], (DIM,), minval=-s, maxval=s), 'Wr': jax.random.uniform(ks[9], (NUM_HEADS - SHARED_HEADS, DIM), minval=-s, maxval=s), 'br': jax.random.uniform(ks[10], (NUM_HEADS - SHARED_HEADS,), minval=-s, maxval=s), 'Ws': jax.random.uniform(ks[11], (2, DIM), minval=-s, maxval=s), 'bs': jax.random.uniform(ks[12], (2,), minval=-s, maxval=s), 'temperature': jnp.full((NUM_HEADS, 1, 1), float(np.log(np.expm1(1.0 / 0.24))), dtype=jnp.float32), 'query_embedding': 0.02 * jax.random.normal(ks[13], (NUM_HEADS, 1, HEAD_DIM), dtype=jnp.float32)}
        return inp
    _L0_ffn_all = _L0_ffn_setup()
    _L0_ffn_in = {k: v for k, v in _L0_ffn_all.items() if k in ('Wq', 'bq', 'Wk', 'bk', 'Wv', 'bv', 'Wp', 'bp', 'Wr', 'br', 'Ws', 'bs', 'temperature', 'query_embedding')}
    del _L0_ffn_all
    return {'x': x, 'ctx_768': ctx_768, 'g_xattn': g_xattn, 'g_ffn': g_ffn, 'L0_xattn_Wq': _L0_xattn_in['Wq'], 'L0_xattn_Wk': _L0_xattn_in['Wk'], 'L0_xattn_Wv': _L0_xattn_in['Wv'], 'L0_xattn_Wo': _L0_xattn_in['Wo'], 'L0_xattn_bo': _L0_xattn_in['bo'], 'L0_ffn_Wq': _L0_ffn_in['Wq'], 'L0_ffn_bq': _L0_ffn_in['bq'], 'L0_ffn_Wk': _L0_ffn_in['Wk'], 'L0_ffn_bk': _L0_ffn_in['bk'], 'L0_ffn_Wv': _L0_ffn_in['Wv'], 'L0_ffn_bv': _L0_ffn_in['bv'], 'L0_ffn_Wp': _L0_ffn_in['Wp'], 'L0_ffn_bp': _L0_ffn_in['bp'], 'L0_ffn_Wr': _L0_ffn_in['Wr'], 'L0_ffn_br': _L0_ffn_in['br'], 'L0_ffn_Ws': _L0_ffn_in['Ws'], 'L0_ffn_bs': _L0_ffn_in['bs'], 'L0_ffn_temperature': _L0_ffn_in['temperature'], 'L0_ffn_query_embedding': _L0_ffn_in['query_embedding']}

def reference(x, ctx_768, g_xattn, g_ffn, L0_xattn_Wq, L0_xattn_Wk, L0_xattn_Wv, L0_xattn_Wo, L0_xattn_bo, L0_ffn_Wq, L0_ffn_bq, L0_ffn_Wk, L0_ffn_bk, L0_ffn_Wv, L0_ffn_bv, L0_ffn_Wp, L0_ffn_bp, L0_ffn_Wr, L0_ffn_br, L0_ffn_Ws, L0_ffn_bs, L0_ffn_temperature, L0_ffn_query_embedding):
    import jax
    import jax.numpy as jnp

    def _L0_xattn_ref(x, context, Wq, Wk, Wv, Wo, bo):
        import jax, jax.numpy as jnp
        import numpy as np
        HEADS = 8
        DIM_HEAD = 64
        SCALE = DIM_HEAD ** (-0.5)
        B, Nq, _ = x.shape
        q = (x @ Wq).reshape(B, Nq, HEADS, DIM_HEAD)
        k = (context @ Wk).reshape(B, context.shape[1], HEADS, DIM_HEAD)
        v = (context @ Wv).reshape(B, context.shape[1], HEADS, DIM_HEAD)
        sim = jnp.einsum('bihd,bjhd->bhij', q, k) * SCALE
        attn = jax.nn.softmax(sim, axis=-1)
        out = jnp.einsum('bhij,bjhd->bihd', attn, v)
        out = out.reshape(B, Nq, HEADS * DIM_HEAD)
        return out @ Wo + bo

    def _L0_ffn_ref(x, Wq, bq, Wk, bk, Wv, bv, Wp, bp, Wr, br, Ws, bs, temperature, query_embedding):
        import jax, jax.numpy as jnp
        import numpy as np
        import math
        DIM = 512
        NUM_HEADS = 16
        SHARED_HEADS = 1
        ROUTED_HEADS = 3
        HEAD_DIM = DIM // NUM_HEADS
        B, N = (2, 1024)
        Bsz, Nn, C = x.shape
        H, hd = (NUM_HEADS, HEAD_DIM)

        def heads(W, b):
            y = x @ W.T + b
            return y.reshape(Bsz, Nn, H, hd).transpose(0, 2, 1, 3)
        q = heads(Wq, bq)
        k = heads(Wk, bk)
        v = heads(Wv, bv)
        q_norm = q / jnp.linalg.norm(q, axis=-1, keepdims=True)
        q_scaled = (q_norm + query_embedding[None]) * jax.nn.softplus(temperature)[None]
        attn = jnp.einsum('bhqd,bhkd->bhqk', q_scaled, k) / math.sqrt(hd)
        attn = jax.nn.softmax(attn, axis=-1)
        h = jnp.einsum('bhqk,bhkd->bhqd', attn, v)
        h = h.transpose(0, 2, 1, 3).reshape(Bsz, Nn, C)
        gates = jax.nn.softmax(h @ Wr.T + br, axis=-1)
        _, idx = jax.lax.top_k(gates, ROUTED_HEADS)
        mask = jax.nn.one_hot(idx, H - SHARED_HEADS, dtype=gates.dtype).sum(axis=-2)
        routed_gates = gates * mask * ROUTED_HEADS
        sw = jax.nn.softmax(h @ Ws.T + bs, axis=-1)
        shared_gates = sw * SHARED_HEADS
        weight_0 = sw * 2.0
        shared_gates = weight_0[..., 0:1] * shared_gates
        routed_gates = weight_0[..., 1:2] * routed_gates
        masked_gates = jnp.concatenate([shared_gates, routed_gates], axis=-1)
        out = h * masked_gates.sum(axis=-1, keepdims=True)
        return out @ Wp.T + bp
    x = x + jnp.tanh(g_xattn[0]) * _L0_xattn_ref(_layernorm(x, axis=-1), ctx_768, L0_xattn_Wq, L0_xattn_Wk, L0_xattn_Wv, L0_xattn_Wo, L0_xattn_bo)
    x = x + jnp.tanh(g_ffn[0]) * _L0_ffn_ref(_layernorm(x, axis=-1), L0_ffn_Wq, L0_ffn_bq, L0_ffn_Wk, L0_ffn_bk, L0_ffn_Wv, L0_ffn_bv, L0_ffn_Wp, L0_ffn_bp, L0_ffn_Wr, L0_ffn_br, L0_ffn_Ws, L0_ffn_bs, L0_ffn_temperature, L0_ffn_query_embedding)
    return x

_drawn_inputs = setup_inputs


def setup_inputs(seed=0):
    import zlib

    import numpy as np

    out = dict(_drawn_inputs(seed))
    spreads = {'L0_ffn_temperature': (4.151041507720947, 0.6)}
    factors = {'L0_xattn_bo': 7.296,
     'L0_ffn_Wq': 5.392,
     'L0_ffn_bq': 8.0,
     'L0_ffn_Wk': 5.39,
     'L0_ffn_bk': 64.0,
     'L0_ffn_bp': 2.689,
     'L0_ffn_Wr': 8.0,
     'L0_ffn_br': 28.231,
     'L0_ffn_Ws': 8.0,
     'L0_ffn_bs': 36.91,
     'L0_ffn_query_embedding': 8.0}
    for name, (base, spread) in spreads.items():
        noise = np.random.default_rng([zlib.crc32(name.encode()), seed]).standard_normal(out[name].shape)
        drawn = base * np.exp(spread * noise) if base else spread * noise
        out[name] = jnp.asarray(drawn.astype(out[name].dtype))
    for name, factor in factors.items():
        out[name] = (out[name] * factor).astype(out[name].dtype)
    return out
```

```python
from contextlib import ExitStack

import concourse.bass as bass
from concourse import mybir

F32 = mybir.dt.float32
F32R = mybir.dt.float32r
ACT = mybir.ActivationFunctionType
ALU = mybir.AluOpType
AX = mybir.AxisListType

B, N, DM, DC = 8, 1024, 512, 384
P = 128
TT = N // P
HALF = N // 2
NG = DM // P
STEPS = 2 * TT
EPS = 1e-5
NE = 15
GC = 18
SH = 16
TOPK = 3


class Phase:

    def __init__(self, ffn):
        self.ffn = ffn
        self.D = 32 if ffn else 64
        self.G = P // self.D
        self.PAIRS = self.G // 2
        self.KC = (DM if ffn else DC) // P
        self.W = 4 if ffn else 0
        self.SCALE = float(self.D) ** -0.5
        self.SLOTS = 2 if ffn else 4
        self.MROW = 96 if ffn else 64
        self.NP = 4 if ffn else 3
        self.SUM = 32 if ffn else 64

    def q_copies(self):
        return [("hi", 0, 0), ("lo", 32, 0), ("hi", 64, 0)] if self.ffn else [("hi", 0, 0), ("lo", 64, 0), ("hi", 0, 1)]

    def k_copies(self):
        return [("hi", 0, 1), ("hi", 32, 1), ("lo", 64, 1)] if self.ffn else [("hi", 0, 2), ("hi", 64, 2), ("lo", 0, 3)]

    def max_operands(self):
        return (0, 1, 96) if self.ffn else (0, 2, 128)

    def score_passes(self):
        return [(1, 0)] if self.ffn else [(2, 0), (3, 1)]

    def m_stack(self):
        return 0 if self.ffn else 1

    def one_stack(self):
        return 1 if self.ffn else 3


def schedule(ph):
    maxima = lambda g: [("mx", g, e, t, j) for e in range(ph.G) for t in range(TT) for j in range(2)]
    queries = lambda g: [[("pq", g, 0)], [("ss", g, 0)], [("pq", g, 1)], [("ss", g, 1)]] if ph.ffn else [[("pq", g, 0)], [("pq", g, 1)]]
    keys = lambda g: [[("pk", g, 0)], [("pk", g, 1)]]
    s = []
    if not ph.ffn:
        s += [("cx", 0)]
    for n in range(2):
        s += [("ln", n)] + [("tr", n, k) for k in range(NG)]
    s += sum(queries(0) + keys(0), []) + [("qd", 0), ("kd", 0)]
    s += [("vp", t) for t in range(TT // 2)]
    s += sum(queries(1) + keys(1), []) + [("qd", 1), ("kd", 1), ("wl", 2), ("wl", 3)]
    m0 = maxima(0)
    per = len(m0) // (TT // 2)
    for t in range(TT // 2, TT):
        s += [("vp", t)] + m0[:per]
        m0 = m0[per:]
    s += m0 + [("wo", 0), ("mt", 0), ("md", 0)]
    s += [("S", 0)]
    for g in range(NG):
        fills = [[] for _ in range(STEPS)]
        if g + 1 < NG:
            m = maxima(g + 1)
            first, end = 2, STEPS - 3
            for i, unit in enumerate(m):
                fills[first + i * (end - first) // len(m)].append(unit)
            fills[end] += [("mt", g + 1), ("md", g + 1)]
        if g + 2 < NG:
            for i, part in enumerate(queries(g + 2) + keys(g + 2)):
                fills[8 + i] += part
        if g == NG - 1:
            for i in range(NG - 1):
                fills[2 + 4 * i].append(("hs", i))
        for st in range(STEPS):
            t = g * STEPS + st
            if t + 1 < NG * STEPS:
                s += [("S", t + 1)]
            s += fills[st] + [("PV", t)]
            if st % TT == TT - 1:
                s += [("ev", g, st // TT)]
        if g + 2 < NG:
            s += [("qd", g + 2), ("kd", g + 2)]
    s += [("hs", NG - 1)]
    if ph.ffn:
        s += [("gt", 0)]
    s += [("op", t) for t in range(TT)]
    return s


AUX_ITEMS = ("tr", "pq", "ss", "pk", "vp", "mx", "mt", "gt", "op")


def count(items, kinds):
    return {it: i for i, it in enumerate([it for it in items if it[0] in kinds])}


def split_weights(nc, weights, w_split):
    with ExitStack() as ctx:
        sb = lambda name, shape, dt: ctx.enter_context(nc.sbuf_tensor(name, shape, dt))
        sem = lambda name: ctx.enter_context(nc.semaphore(name))
        raw = sb("w_raw", [P, NG, DM], F32)
        hi = sb("w_hi", [P, NG, DM], F32R)
        lo = sb("w_lo", [P, NG, DM], F32R)
        raw_in, hi_ok, lo_ok, out_ok = sem("w_raw_in"), sem("w_hi_ok"), sem("w_lo_ok"), sem("w_out_ok")
        with nc.Fori(0, 8) as w:
            with nc.Block() as block:

                @block.sync
                def _(sp):
                    sp.dma_start(raw[:], weights[bass.ds(w, 1)].rearrange("a (k p) c -> p (a k) c", p=P)).then_inc(raw_in, 16)
                    sp.wait_ge(lo_ok, 1)
                    for part, src in enumerate((hi, lo)):
                        for g in range(NG):
                            sp.dma_start(w_split[bass.ds(w, 1), part, g].rearrange("a p k c -> p (a k) c"),
                                         src[:, :, g * P:(g + 1) * P].bitcast(F32)).then_inc(out_ok, 16)
                    sp.wait_ge(out_ok, 2 * NG * 16)

                @block.scalar
                def _(act):
                    act.wait_ge(raw_in, 16)
                    act.activation(hi[:], raw[:], ACT.Copy).then_inc(hi_ok, 1)

                @block.vector
                def _(dve):
                    dve.wait_ge(raw_in, 16)
                    dve.wait_ge(hi_ok, 1)
                    dve.tensor_tensor(lo[:], raw[:], hi[:].bitcast(F32), ALU.subtract).then_inc(lo_ok, 1)

            for s in (raw_in, hi_ok, lo_ok, out_ok):
                nc.sync.sem_clear(s)
            nc.all_engine_barrier()


def attention_phase(nc, ph, x_in, ctxT, w_split, bias_row, gate_scalar, x_out, small):
    ffn, D, G, PAIRS, KC = ph.ffn, ph.D, ph.G, ph.PAIRS, ph.KC
    SCHED = schedule(ph)
    USE = count(SCHED, AUX_ITEMS)
    HI = count(SCHED, ("tr", "pk") if ffn else ("tr", "pk", "pq"))
    QN = count(SCHED, ("pq",))
    MX = count(SCHED, ("mx",))
    last = lambda kind: max(USE[it] for it in USE if it[0] == kind)
    NCOPY = G * 3
    pre = "f_" if ffn else "x_"
    with ExitStack() as ctx:
        sb = lambda name, shape, dt=F32: ctx.enter_context(nc.sbuf_tensor(pre + name, shape, dt))
        made = []

        def sem(name, cleared=True):
            s = ctx.enter_context(nc.semaphore(pre + name))
            if cleared:
                made.append(s)
            return s

        xh = sb("xh", [P, TT, DM])
        hT = xh[:].rearrange("p (g a) d -> p g (a d)", g=NG)
        xT_hi = sb("xT_hi", [P, NG, N], F32R)
        xT_lo = sb("xT_lo", [P, NG, N], F32R)
        if ffn:
            kv_hi, kv_lo = xT_hi, xT_lo
        else:
            kv_hi = sb("kv_hi", [P, KC, N], F32R)
            kv_lo = sb("kv_lo", [P, KC, N], F32R)
        wqk = sb("wqk", [P, 2, 2, 2, NG, P], F32R)
        wvo = sb("wvo", [P, 2, NG, NG, P], F32R)
        stack = sb("stack", [P, 2, G * ph.SLOTS, N], F32R)
        cq = {h: sb(f"cq_{h}", [P, N], F32R) for h in ("hi", "lo")}
        ck = {h: sb(f"ck_{h}", [P, N], F32R) for h in ("hi", "lo")}
        v = sb("v", [P, TT, DM])
        probs = sb("probs", [P, ph.NP, 2 * HALF])
        xo = probs[:].rearrange("p a (b c) -> p (a b) c", c=DM)
        NXO = 2 * ph.NP
        rn = sb("rn", [P, HALF])
        rn2 = sb("rn2", [P, HALF])
        mx = sb("mx", [P, G * TT, 2])
        nm = sb("nm", [P, G * TT])
        mrow = sb("mrow", [G * TT, P], F32R)
        ident = sb("ident", [P, P])
        ones = sb("ones", [P, ph.SUM])
        bo = sb("bo", [P, DM])
        tg = sb("tg", [P, 1])
        st = sb("st", [P, TT, 6])
        mv = sb("mv", [P, TT, 2])
        rs = sb("rs", [P, 3, TT])
        if ffn:
            qb = sb("qb", [P, 2, HALF])
            sq = sb("sq", [P, 2, HALF])
            qy = sb("qy", [P, 2, HALF])
            blk = sb("blk", [P, P])
            bq, bk = sb("bq", [P, NG]), sb("bk", [P, NG])
            emb, tau, et = sb("emb", [P, NG]), sb("tau", [P, NG]), sb("et", [P, NG])
            tmp = sb("tmp", [P, 3, NG])
            bv = sb("bv", [P, DM])
            wg = sb("wg", [P, NG, GC])
            wg_hi, wg_lo = sb("wg_hi", [P, NG, GC], F32R), sb("wg_lo", [P, NG, GC], F32R)
            bg = sb("bg", [P, GC])
            lg = sb("lg", [P, TT, GC])
            eg = sb("eg", [P, TT, GC])
            gm = sb("gm", [P, TT, 2])
            top = sb("top", [P, TT, 8])
            g1 = sb("g1", [P, 4, TT])
            sw = sb("sw", [P, TT, 2])
            sc = sb("sc", [P, TT])
        acc = ctx.enter_context(nc.psum_tensor(pre + "acc", [P, HALF], F32))
        sums = ctx.enter_context(nc.psum_tensor(pre + "sums", [P, HALF], F32))
        scores = ctx.enter_context(nc.psum_tensor(pre + "scores", [P, 2, 2 * HALF], F32))
        aux = ctx.enter_context(nc.psum_tensor(pre + "aux", [P, 2, HALF], F32))

        c_in, c_ms, c_act, c_dve = (sem(n, False) for n in ("c_in", "c_ms", "c_act", "c_dve"))
        c_abs = sem("c_abs", False)
        n_const = 2 + (2 + 3 + 1 + G if ffn else 0)
        with nc.Block() as block:

            @block.sync
            def _(sp):
                sp.dma_start(tg[:], gate_scalar.partition_broadcast(P)).then_inc(c_in, 16)
                sp.dma_start(bo[:], bias_row.partition_broadcast(P)).then_inc(c_in, 16)
                if ffn:
                    sp.dma_start(bv[:], small["bv"].partition_broadcast(P)).then_inc(c_in, 16)
                    sp.dma_start(bg[:], small["bg"].partition_broadcast(P)).then_inc(c_in, 16)
                    for dst, name in ((bq, "bq"), (bk, "bk"), (emb, "emb")):
                        sp.dma_start(dst[:], small[name]).then_inc(c_in, 16)
                    sp.dma_start(wg[:], small["wg"].rearrange("(k p) c -> p k c", p=P)).then_inc(c_in, 16)
                    for e in range(G):
                        sp.dma_start(tau[e * D:(e + 1) * D, :], small["temp"][e].partition_broadcast(D)).then_inc(c_in, 16)

            @block.gpsimd
            def _(pool):
                pool.memset(ident[:], 0.0).then_inc(c_ms, 1)
                pool.memset(ones[:], 1.0).then_inc(c_ms, 1)
                pool.wait_ge(c_ms, 2)
                pool.affine_select(out=ident[:], in_=ident[:], compare_op=ALU.not_equal, fill=1.0, base=0,
                                   pattern=[[-1, P]], channel_multiplier=1).then_inc(c_ms, 1)

            @block.vector
            def _(dve):
                done = [0]

                def link(ins):
                    done[0] += 1
                    ins.then_inc(c_dve, 1)
                    dve.wait_ge(c_dve, done[0])

                for par in range(2):
                    for e in range(G):
                        for slot in (ph.m_stack(), ph.one_stack()):
                            link(dve.memset(stack[ph.MROW:P, par, e * ph.SLOTS + slot, :].bitcast(F32), 0.0))
                        link(dve.memset(stack[ph.MROW:ph.MROW + 1, par, e * ph.SLOTS + ph.one_stack(), :].bitcast(F32), 1.0))
                if ffn:
                    link(dve.memset(blk[:], 0.0))
                    for e in range(G):
                        link(dve.memset(blk[e * D:(e + 1) * D, e * D:(e + 1) * D], 1.0))
                dve.wait_ge(c_act, 1)
                link(dve.tensor_scalar(bo[:], bo[:], tg[:, 0:1], None, ALU.mult))
                if ffn:
                    link(dve.tensor_scalar(tmp[:, 0], tau[:], -1.0, None, ALU.mult))
                    dve.tensor_tensor(tmp[:, 0], tau[:], tmp[:, 0], ALU.min).then_inc(c_abs, 1)
                    dve.wait_ge(c_act, 3)
                    link(dve.tensor_scalar(tau[:], tau[:], 0.0, None, ALU.max))
                    link(dve.tensor_tensor(tau[:], tau[:], tmp[:, 2], ALU.add))
                    link(dve.tensor_tensor(et[:], emb[:], tau[:], ALU.mult))
                    link(dve.tensor_copy(wg_hi[:], wg[:]))
                    link(dve.tensor_tensor(wg_lo[:], wg[:], wg_hi[:].bitcast(F32), ALU.subtract))

            @block.scalar
            def _(act):
                act.wait_ge(c_in, 16 * n_const)
                act.activation(tg[:], tg[:], ACT.Tanh).then_inc(c_act, 1)
                act.preload_act_table_set("natural_log_exp_and_others")
                if ffn:
                    act.wait_ge(c_abs, 1)
                    act.activation(tmp[:, 1], tmp[:, 0], ACT.Exp).then_inc(c_act, 1)
                    act.wait_ge(c_act, 2)
                    act.activation(tmp[:, 2], tmp[:, 1], ACT.Ln, bias=1.0).then_inc(c_act, 1)

        x_loaded, ctx_loaded, wv_loaded, wo_loaded = sem("x_loaded"), sem("ctx_loaded"), sem("wv_loaded"), sem("wo_loaded")
        w_loaded = [sem(f"w_loaded{i}") for i in range(2)]
        q_stacked = [sem(f"q_stacked{i}") for i in range(2)]
        k_stacked = [sem(f"k_stacked{i}") for i in range(2)]
        m_stacked = [sem(f"m_stacked{i}") for i in range(2)]
        xo_loaded = [sem(f"xo_loaded{i}") for i in range(TT)]
        stored = [sem(f"stored{i}") for i in range(TT)]
        ctx_hi_ok, ctx_lo_ok = sem("ctx_hi_ok"), sem("ctx_lo_ok")
        normed = sem("normed")
        rstd_in, rstd_ok = sem("rstd_in"), sem("rstd_ok")
        aux_full, aux_drained = sem("aux_full"), sem("aux_drained")
        hi_ok = sem("hi_ok")
        sq_ok, y_ok, qn_ok, qs_ok, qlo_ok = (sem(n) for n in ("sq_ok", "y_ok", "qn_ok", "qs_ok", "qlo_ok"))
        nm_ok = sem("nm_ok")
        scored, probs_ok, weighed = sem("scored"), sem("probs_ok"), sem("weighed")
        rinv_ok, acc_free = sem("rinv_ok"), sem("acc_free")
        h_hi_ok, h_lo_ok = sem("h_hi_ok"), sem("h_lo_ok")
        gates_in, gates_exp, gates_ok = sem("gates_in"), sem("gates_exp"), sem("gates_ok")
        act_chain, dve_chain = sem("act_chain"), sem("dve_chain")

        def w_tile(what, part, g, k):
            return wqk[:, g % 2, what, part, k, :]

        with nc.Fori(0, B) as b:
            with nc.Block() as block:

                @block.sync
                def _(sp):
                    sp.dma_start(xh[:], x_in[bass.ds(b, 1)].rearrange("a (t p) d -> p (a t) d", p=P)).then_inc(x_loaded, 16)
                    if not ffn:
                        raw = probs[:, 0:3, :]
                        sp.dma_start(raw, ctxT[bass.ds(b, 1)].rearrange("a (k p) n -> p (a k) n", p=P)).then_inc(ctx_loaded, 16)

                    def load_qk(g):
                        for what in range(2):
                            for part in range(2):
                                sp.dma_start(wqk[:, g % 2, what, part].bitcast(F32), w_split[ph.W + what, part, g]).then_inc(w_loaded[g % 2], 16)

                    def load_full(w, done):
                        for part in range(2):
                            sp.dma_start(wvo[:, part].bitcast(F32), w_split[w, part].rearrange("g p k c -> p k g c")).then_inc(done, 16)

                    load_qk(0)
                    load_full(ph.W + 2, wv_loaded)
                    load_qk(1)
                    for it in SCHED:
                        kind, g = it[0], it[1]
                        if kind == "wl":
                            sp.wait_ge(aux_full, USE[("pk", g - 2, 1)] + 1)
                            load_qk(g)
                        elif kind == "wo":
                            sp.wait_ge(aux_full, USE[("vp", TT - 1)] + 1)
                            load_full(ph.W + 3, wo_loaded)
                        elif kind in ("qd", "kd"):
                            if g >= 2:
                                sp.wait_ge(scored, STEPS * PAIRS * (g - 1))
                            if kind == "qd" and ffn:
                                sp.wait_ge(qlo_ok, 2 * (g + 1))
                            else:
                                sp.wait_ge(aux_drained, USE[("pq" if kind == "qd" else "pk", g, 1)] + 1)
                            src, copies, done = (cq, ph.q_copies(), q_stacked) if kind == "qd" else (ck, ph.k_copies(), k_stacked)
                            for e in range(G):
                                for half, row, slot in copies:
                                    sp.dma_start(stack[row:row + D, g % 2, e * ph.SLOTS + slot, :].bitcast(F32),
                                                 src[half][e * D:(e + 1) * D, :].bitcast(F32)).then_inc(done[g % 2], 16)
                        elif kind == "md":
                            sp.wait_ge(aux_drained, USE[("mt", g)] + 1)
                            for e in range(G):
                                dst = stack[ph.MROW:ph.MROW + 1, g % 2, e * ph.SLOTS + ph.m_stack(), :]
                                sp.dma_start(dst.rearrange("o (t q) -> o t q", q=P).bitcast(F32),
                                             mrow[e * TT:(e + 1) * TT, :].bitcast(F32)).then_inc(m_stacked[g % 2], 16)
                    sp.wait_ge(weighed, NG * STEPS)
                    xb = x_in[bass.ds(b, 1)].rearrange("a (t p) d -> p (a t) d", p=P)
                    ob = x_out[bass.ds(b, 1)].rearrange("a (t p) d -> p (a t) d", p=P)
                    for t in range(min(NXO, TT)):
                        sp.dma_start(xo[:, t, :], xb[:, t, :]).then_inc(xo_loaded[t], 16)
                    for t in range(TT):
                        sp.wait_ge(aux_drained, USE[("op", t)] + 1)
                        sp.dma_start(ob[:, t, :], xo[:, t % NXO, :]).then_inc(stored[t], 16)
                        if t + NXO < TT:
                            sp.wait_ge(stored[t], 16)
                            sp.dma_start(xo[:, t, :], xb[:, t + NXO, :]).then_inc(xo_loaded[t + NXO], 16)
                    for t in range(TT):
                        sp.wait_ge(stored[t], 16)

                @block.gpsimd
                def _(pool):
                    for it in SCHED:
                        kind = it[0]
                        if kind == "cx":
                            pool.wait_ge(ctx_loaded, 16)
                            for k in range(KC):
                                pool.wait_ge(ctx_hi_ok, k + 1)
                                pool.tensor_tensor(kv_lo[:, k, :], probs[:, k, :], kv_hi[:, k, :].bitcast(F32),
                                                   ALU.subtract).then_inc(ctx_lo_ok, 1)
                        elif kind == "ss":
                            _, g, n = it
                            pool.wait_ge(qs_ok, 2 * (2 * g + n) + 2)
                            q = slice(n * HALF, (n + 1) * HALF)
                            pool.tensor_tensor(cq["lo"][:, q], qy[:, n], cq["hi"][:, q].bitcast(F32), ALU.subtract).then_inc(qlo_ok, 1)
                        elif kind == "hs":
                            g = it[1]
                            pool.wait_ge(h_hi_ok, g + 1)
                            pool.tensor_tensor(xT_lo[:, g, :], hT[:, g, :], xT_hi[:, g, :].bitcast(F32), ALU.subtract).then_inc(h_lo_ok, 1)

                @block.tensor
                def _(pe):
                    def bank(it):
                        u = USE[it]
                        if u >= 2:
                            pe.wait_ge(aux_drained, u - 1)
                        return aux[:, u % 2, :]

                    def product(out, lhs, rhs, tiles):
                        terms = [(k, a, c) for k in range(tiles) for a, c in ((0, 0), (0, 1), (1, 0))]
                        for i, (k, a, c) in enumerate(terms):
                            ins = pe.matmul(out, lhs(a, k), rhs(c, k), start=i == 0, stop=i == len(terms) - 1)
                        return ins

                    xT, kvT = (xT_hi, xT_lo), (kv_hi, kv_lo)
                    for it in SCHED:
                        kind = it[0]
                        if kind == "tr":
                            _, n, k = it
                            pe.wait_ge(normed, n + 1)
                            out = bank(it)
                            for i in range(TT // 2):
                                ins = pe.transpose(out[:, i * P:(i + 1) * P], xh[:, n * TT // 2 + i, k * P:(k + 1) * P], ident[:])
                            ins.then_inc(aux_full, 1)
                        elif kind in ("pq", "pk"):
                            _, g, n = it
                            what = int(kind == "pk")
                            pe.wait_ge(w_loaded[g % 2], 64 * (g // 2 + 1))
                            if what and not ffn:
                                pe.wait_ge(ctx_lo_ok, KC)
                            else:
                                pe.wait_ge(aux_drained, USE[("tr", 1, NG - 1)] + 1)
                            src = kvT if what else xT
                            q = slice(n * HALF, (n + 1) * HALF)
                            product(bank(it), lambda a, k: w_tile(what, a, g, k), lambda c, k: src[c][:, k, q],
                                    KC if what else NG).then_inc(aux_full, 1)
                        elif kind == "ss":
                            _, g, n = it
                            out = bank(it)
                            pe.wait_ge(sq_ok, 2 * g + n + 1)
                            pe.matmul(out, blk[:], sq[:, n], start=True, stop=True).then_inc(aux_full, 1)
                        elif kind == "vp":
                            t = it[1]
                            pe.wait_ge(wv_loaded, 32)
                            if ffn:
                                pe.wait_ge(aux_drained, USE[("tr", 1, NG - 1)] + 1)
                            else:
                                pe.wait_ge(ctx_lo_ok, KC)
                            r = slice(t * P, (t + 1) * P)
                            product(bank(it), lambda a, k: kvT[a][:, k, r], lambda c, k: wvo[:, c, k].rearrange("p g c -> p (g c)"),
                                    KC).then_inc(aux_full, 1)
                        elif kind == "mx":
                            _, g, e, t, j = it
                            qs, ks, rows = ph.max_operands()
                            out = bank(it)
                            pe.wait_ge(q_stacked[g % 2], NCOPY * 16 * (g // 2 + 1))
                            pe.wait_ge(k_stacked[g % 2], NCOPY * 16 * (g // 2 + 1))
                            pe.matmul(out, stack[0:rows, g % 2, e * ph.SLOTS + qs, t * P:(t + 1) * P],
                                      stack[0:rows, g % 2, e * ph.SLOTS + ks, j * HALF:(j + 1) * HALF],
                                      start=True, stop=True).then_inc(aux_full, 1)
                        elif kind == "mt":
                            g = it[1]
                            out = bank(it)
                            pe.wait_ge(nm_ok, g + 1)
                            pe.transpose(out[0:G * TT, 0:P], nm[:], ident[:]).then_inc(aux_full, 1)
                        elif kind == "S":
                            g, s = divmod(it[1], STEPS)
                            n, jt = divmod(s, TT)
                            if s == 0:
                                pe.wait_ge(m_stacked[g % 2], G * 16 * (g // 2 + 1))
                            for pair in range(PAIRS):
                                u = it[1] * PAIRS + pair
                                if u >= 2:
                                    pe.wait_ge(probs_ok, u - 1)
                                for i in range(2):
                                    e = 2 * pair + i
                                    passes = ph.score_passes()
                                    for a, (ks, qs) in enumerate(passes):
                                        ins = pe.matmul(scores[:, u % 2, i * HALF:(i + 1) * HALF],
                                                        stack[:, g % 2, e * ph.SLOTS + ks, jt * P:(jt + 1) * P],
                                                        stack[:, g % 2, e * ph.SLOTS + qs, n * HALF:(n + 1) * HALF],
                                                        start=a == 0, stop=a == len(passes) - 1)
                                ins.then_inc(scored, 1)
                        elif kind == "PV":
                            g, s = divmod(it[1], STEPS)
                            n, jt = divmod(s, TT)
                            pe.wait_ge(probs_ok, (it[1] + 1) * PAIRS)
                            if it[1] == 0:
                                pe.wait_ge(aux_drained, USE[("vp", TT - 1)] + 1)
                            if jt == 0 and (g or n):
                                pe.wait_ge(acc_free, 2 * g + n)
                            for e in range(G):
                                u = it[1] * PAIRS + e // 2
                                pe.matmul(acc[e * D:(e + 1) * D, :], v[:, jt, g * P + e * D:g * P + (e + 1) * D],
                                          probs[:, u % ph.NP, (e % 2) * HALF:(e % 2 + 1) * HALF], start=jt == 0, stop=jt == TT - 1)
                            for e in range(G):
                                u = it[1] * PAIRS + e // 2
                                ins = pe.matmul(sums[e * D:(e + 1) * D, :], ones[:], probs[:, u % ph.NP, (e % 2) * HALF:(e % 2 + 1) * HALF],
                                                start=jt == 0, stop=jt == TT - 1)
                            ins.then_inc(weighed, 1)
                        elif kind == "gt":
                            out = bank(it)
                            pe.wait_ge(h_lo_ok, NG)
                            for t in range(TT):
                                r = slice(t * P, (t + 1) * P)
                                ins = product(out[:, t * GC:(t + 1) * GC], lambda a, k: xT[a][:, k, r],
                                              lambda c, k: (wg_hi, wg_lo)[c][:, k, :], NG)
                            ins.then_inc(aux_full, 1)
                        elif kind == "op":
                            t = it[1]
                            out = bank(it)
                            pe.wait_ge(wo_loaded, 32)
                            pe.wait_ge(h_lo_ok, NG)
                            r = slice(t * P, (t + 1) * P)
                            product(out, lambda a, k: xT[a][:, k, r], lambda c, k: wvo[:, c, k].rearrange("p g c -> p (g c)"),
                                    NG).then_inc(aux_full, 1)

                @block.scalar
                def _(act):
                    chain = [0]

                    def link(ins):
                        chain[0] += 1
                        ins.then_inc(act_chain, 1)
                        act.wait_ge(act_chain, chain[0])

                    for it in SCHED:
                        kind = it[0]
                        if kind == "cx":
                            act.wait_ge(ctx_loaded, 16)
                            for k in range(KC):
                                act.activation(kv_hi[:, k, :], probs[:, k, :], ACT.Copy).then_inc(ctx_hi_ok, 1)
                        elif kind == "ln":
                            n = it[1]
                            r = slice(n * TT // 2, (n + 1) * TT // 2)
                            act.wait_ge(rstd_in, n + 1)
                            link(act.activation(rs[:, 1, r], rs[:, 0, r], ACT.Ln))
                            act.activation(rs[:, 1, r], rs[:, 1, r], ACT.Exp, scale=-0.5).then_inc(rstd_ok, 1)
                        elif kind == "tr":
                            _, n, k = it
                            act.wait_ge(aux_full, USE[it] + 1)
                            act.activation(xT_hi[:, k, n * HALF:(n + 1) * HALF], aux[:, USE[it] % 2, :], ACT.Copy).then_inc(hi_ok, 1)
                        elif kind == "pk" or (kind == "pq" and not ffn):
                            _, g, n = it
                            if g and n == 0:
                                act.wait_ge((q_stacked if kind == "pq" else k_stacked)[(g - 1) % 2], NCOPY * 16 * ((g - 1) // 2 + 1))
                            act.wait_ge(aux_full, USE[it] + 1)
                            dst = (cq if kind == "pq" else ck)["hi"][:, n * HALF:(n + 1) * HALF]
                            if ffn:
                                act.activation(dst, aux[:, USE[it] % 2, :], ACT.Identity, bias=bk[:, g:g + 1]).then_inc(hi_ok, 1)
                            else:
                                act.activation(dst, aux[:, USE[it] % 2, :], ACT.Copy).then_inc(hi_ok, 1)
                        elif kind == "pq":
                            _, g, n = it
                            act.wait_ge(aux_drained, USE[it] + 1)
                            act.activation(sq[:, n], qb[:, n], ACT.Square).then_inc(sq_ok, 1)
                        elif kind == "ss":
                            _, g, n = it
                            i = 2 * g + n
                            if g:
                                act.wait_ge(qlo_ok, i - 1)
                            act.wait_ge(aux_full, USE[it] + 1)
                            link(act.activation(qy[:, n], aux[:, USE[it] % 2, :], ACT.Ln))
                            link(act.activation(qy[:, n], qy[:, n], ACT.Exp, scale=-0.5))
                            act.activation(sq[:, n], qy[:, n], ACT.Square).then_inc(y_ok, 1)
                            act.wait_ge(qn_ok, i + 1)
                            act.activation(qy[:, n], qb[:, n], ACT.Identity, scale=tau[:, g:g + 1], bias=et[:, g:g + 1]).then_inc(qs_ok, 1)
                            act.wait_ge(qs_ok, 2 * i + 1)
                            if g and n == 0:
                                act.wait_ge(q_stacked[(g - 1) % 2], NCOPY * 16 * ((g - 1) // 2 + 1))
                            act.activation(cq["hi"][:, n * HALF:(n + 1) * HALF], qy[:, n], ACT.Copy).then_inc(qs_ok, 1)
                        elif kind == "S":
                            for pair in range(PAIRS):
                                u = it[1] * PAIRS + pair
                                act.wait_ge(scored, u + 1)
                                if u >= ph.NP:
                                    act.wait_ge(weighed, (u - ph.NP) // PAIRS + 1)
                                elif not ffn:
                                    act.wait_ge(ctx_lo_ok, KC)
                                act.activation(probs[:, u % ph.NP, :], scores[:, u % 2, :], ACT.Exp, scale=ph.SCALE).then_inc(probs_ok, 1)
                        elif kind == "ev":
                            _, g, n = it
                            i = 2 * g + n
                            act.wait_ge(weighed, TT * (i + 1))
                            if i:
                                act.wait_ge(acc_free, i)
                            link(act.activation(rn[:], sums[:], ACT.Ln))
                            act.activation(rn[:], rn[:], ACT.Exp, scale=-1.0).then_inc(rinv_ok, 1)
                        elif kind == "hs":
                            g = it[1]
                            act.wait_ge(acc_free, 2 * g + 2)
                            act.activation(xT_hi[:, g, :], hT[:, g, :], ACT.Copy).then_inc(h_hi_ok, 1)
                        elif kind == "gt":
                            act.wait_ge(gates_in, 1)
                            act.activation(eg[:], lg[:], ACT.Exp).then_inc(gates_exp, 1)

                @block.vector
                def _(dve):
                    chain = [0]

                    def link(ins):
                        chain[0] += 1
                        ins.then_inc(dve_chain, 1)
                        dve.wait_ge(dve_chain, chain[0])

                    def full(it):
                        dve.wait_ge(aux_full, USE[it] + 1)
                        return aux[:, USE[it] % 2, :]

                    def newton(y, x, y2, out):
                        link(dve.scalar_tensor_tensor(y2, y2, -0.5, x, ALU.mult, ALU.mult))
                        return dve.scalar_tensor_tensor(out, y2, 1.5, y, ALU.add, ALU.mult)

                    for it in SCHED:
                        kind = it[0]
                        if kind == "ln":
                            n = it[1]
                            tiles = range(n * TT // 2, (n + 1) * TT // 2)
                            r = slice(n * TT // 2, (n + 1) * TT // 2)
                            dve.wait_ge(x_loaded, 16)
                            for t in tiles:
                                ins = dve.bn_stats(st[:, t, :], xh[:, t, :])
                            link(ins)
                            for t in tiles:
                                ins = dve.bn_aggr(mv[:, t, :], st[:, t, :])
                            link(ins)
                            dve.tensor_scalar(rs[:, 0, r], mv[:, r, 1], EPS, None, ALU.add).then_inc(rstd_in, 1)
                            dve.wait_ge(rstd_in, n + 1)
                            dve.wait_ge(rstd_ok, n + 1)
                            link(dve.tensor_tensor(rs[:, 2, r], rs[:, 1, r], rs[:, 1, r], ALU.mult))
                            link(newton(rs[:, 1, r], rs[:, 0, r], rs[:, 2, r], rs[:, 1, r]))
                            for t in tiles:
                                ins = dve.tensor_scalar(xh[:, t, :], xh[:, t, :], mv[:, t, 0:1], rs[:, 1, t:t + 1], ALU.subtract, ALU.mult)
                            ins.then_inc(normed, 1)
                        elif kind == "tr":
                            _, n, k = it
                            src = full(it)
                            q = slice(n * HALF, (n + 1) * HALF)
                            dve.wait_ge(hi_ok, HI[it] + 1)
                            dve.tensor_tensor(xT_lo[:, k, q], src, xT_hi[:, k, q].bitcast(F32), ALU.subtract).then_inc(aux_drained, 1)
                        elif kind == "pk" or (kind == "pq" and not ffn):
                            _, g, n = it
                            src = full(it)
                            q = slice(n * HALF, (n + 1) * HALF)
                            c = cq if kind == "pq" else ck
                            dve.wait_ge(hi_ok, HI[it] + 1)
                            if ffn:
                                ins = dve.scalar_tensor_tensor(c["lo"][:, q], src, bk[:, g:g + 1], c["hi"][:, q].bitcast(F32), ALU.add, ALU.subtract)
                            else:
                                ins = dve.tensor_tensor(c["lo"][:, q], src, c["hi"][:, q].bitcast(F32), ALU.subtract)
                            ins.then_inc(aux_drained, 1)
                        elif kind == "pq":
                            _, g, n = it
                            src = full(it)
                            if g:
                                dve.wait_ge(qs_ok, 2 * (2 * (g - 1) + n) + 1)
                            dve.tensor_scalar(qb[:, n], src, bq[:, g:g + 1], None, ALU.add).then_inc(aux_drained, 1)
                        elif kind == "ss":
                            _, g, n = it
                            src = full(it)
                            dve.wait_ge(y_ok, 2 * g + n + 1)
                            dve.scalar_tensor_tensor(sq[:, n], sq[:, n], -0.5, src, ALU.mult, ALU.mult).then_inc(aux_drained, 1)
                            dve.wait_ge(aux_drained, USE[it] + 1)
                            link(dve.scalar_tensor_tensor(qy[:, n], sq[:, n], 1.5, qy[:, n], ALU.add, ALU.mult))
                            dve.tensor_tensor(qb[:, n], qb[:, n], qy[:, n], ALU.mult).then_inc(qn_ok, 1)
                        elif kind == "vp":
                            t = it[1]
                            src = full(it)
                            if ffn:
                                dve.tensor_tensor(v[:, t, :], src, bv[:], ALU.add).then_inc(aux_drained, 1)
                            else:
                                dve.tensor_copy(v[:, t, :], src).then_inc(aux_drained, 1)
                        elif kind == "mx":
                            _, g, e, t, j = it
                            src = full(it)
                            dve.tensor_reduce(mx[:, e * TT + t, j:j + 1], src, axis=AX.X, op=ALU.max).then_inc(aux_drained, 1)
                        elif kind == "mt":
                            g = it[1]
                            dve.wait_ge(aux_drained, USE[it])
                            dve.tensor_reduce(nm[:], mx[:], axis=AX.X, op=ALU.max, negate=True).then_inc(nm_ok, 1)
                            src = full(it)
                            if g:
                                dve.wait_ge(m_stacked[(g - 1) % 2], G * 16 * ((g - 1) // 2 + 1))
                            dve.tensor_copy(mrow[:], src[0:G * TT, 0:P]).then_inc(aux_drained, 1)
                        elif kind == "ev":
                            _, g, n = it
                            dve.wait_ge(rinv_ok, 2 * g + n + 1)
                            link(dve.scalar_tensor_tensor(rn2[:], sums[:], -1.0, rn[:], ALU.mult, ALU.mult))
                            link(dve.scalar_tensor_tensor(rn[:], rn2[:], 2.0, rn[:], ALU.add, ALU.mult))
                            dve.tensor_tensor(hT[:, g, n * HALF:(n + 1) * HALF], acc[:], rn[:], ALU.mult).then_inc(acc_free, 1)
                        elif kind == "gt":
                            src = full(it)
                            for t in range(TT):
                                ins = dve.tensor_tensor(lg[:, t, :], src[:, t * GC:(t + 1) * GC], bg[:], ALU.add)
                            ins.then_inc(aux_drained, 1)
                            dve.wait_ge(aux_drained, USE[it] + 1)
                            dve.tensor_reduce(gm[:, :, 0], lg[:, :, 0:NE], axis=AX.X, op=ALU.max)
                            link(dve.tensor_reduce(gm[:, :, 1], lg[:, :, SH:SH + 2], axis=AX.X, op=ALU.max))
                            dve.tensor_tensor(lg[:, :, 0:NE], lg[:, :, 0:NE], gm[:, :, 0:1].to_broadcast([P, TT, NE]), ALU.subtract)
                            dve.tensor_tensor(lg[:, :, SH:SH + 2], lg[:, :, SH:SH + 2], gm[:, :, 1:2].to_broadcast([P, TT, 2]), ALU.subtract).then_inc(gates_in, 1)
                            dve.wait_ge(gates_exp, 1)
                            for t in range(TT):
                                dve.max(top[:, t, :], eg[:, t, 0:NE])
                            dve.tensor_reduce(g1[:, 0], eg[:, :, 0:NE], axis=AX.X, op=ALU.add)
                            link(dve.tensor_reduce(g1[:, 1], eg[:, :, SH:SH + 2], axis=AX.X, op=ALU.add))
                            link(dve.tensor_reduce(g1[:, 2], top[:, :, 0:TOPK], axis=AX.X, op=ALU.add))
                            link(dve.reciprocal(g1[:, 0:2], g1[:, 0:2]))
                            dve.tensor_tensor(g1[:, 2], g1[:, 2], g1[:, 0], ALU.mult)
                            dve.tensor_tensor(sw[:, :, 0], eg[:, :, SH], g1[:, 1], ALU.mult)
                            link(dve.tensor_tensor(sw[:, :, 1], eg[:, :, SH + 1], g1[:, 1], ALU.mult))
                            link(dve.tensor_tensor(g1[:, 3], sw[:, :, 0], sw[:, :, 1], ALU.add))
                            dve.scalar_tensor_tensor(g1[:, 0], g1[:, 3], 2.0, sw[:, :, 0], ALU.mult, ALU.mult)
                            link(dve.scalar_tensor_tensor(g1[:, 1], g1[:, 2], 2.0 * TOPK, sw[:, :, 1], ALU.mult, ALU.mult))
                            link(dve.tensor_tensor(g1[:, 0], g1[:, 0], g1[:, 1], ALU.add))
                            link(dve.tensor_scalar(sc[:], g1[:, 0], tg[:, 0:1], None, ALU.mult))
                        elif kind == "op":
                            t = it[1]
                            s = t % NXO
                            dve.wait_ge(xo_loaded[t], 16)
                            link(dve.tensor_tensor(xo[:, s, :], xo[:, s, :], bo[:], ALU.add))
                            src = full(it)
                            by = sc[:, t:t + 1] if ffn else tg[:, 0:1]
                            dve.scalar_tensor_tensor(xo[:, s, :], src, by, xo[:, s, :], ALU.mult, ALU.add).then_inc(aux_drained, 1)

            for s in made:
                nc.sync.sem_clear(s)
            nc.all_engine_barrier()
        for s in (c_in, c_ms, c_act, c_dve, c_abs):
            nc.sync.sem_clear(s)
        nc.all_engine_barrier()


def build(nc, x, ctxT, weights, g_xattn, g_ffn, xattn_bo, bq, bk, bv, bp, wg, bg, temp, emb, out):
    w_split = nc.dram_tensor("w_split", [8, 2, NG, P, NG, P], F32).ap()
    x1 = nc.dram_tensor("x_after_xattn", [B, N, DM], F32).ap()
    split_weights(nc, weights, w_split)
    attention_phase(nc, Phase(False), x, ctxT, w_split, xattn_bo, g_xattn, x1, {})
    attention_phase(nc, Phase(True), x1, None, w_split, bp, g_ffn, out,
                    dict(bq=bq, bk=bk, bv=bv, wg=wg, bg=bg, temp=temp, emb=emb))


def kernel(**inputs):
    import numpy as np
    import concourse.bacc as bacc
    from concourse.bass_utils import run_bass_kernel_spmd

    a = {k: np.asarray(v) for k, v in inputs.items()}
    pad = lambda w: np.concatenate([w, np.zeros((DM - w.shape[0], DM), w.dtype)]) if w.shape[0] < DM else w
    channels = lambda v: np.ascontiguousarray(v.reshape(NG, P).T)
    zero = np.zeros(1, np.float32)
    arrays = {
        "x": a["x"],
        "ctxT": np.ascontiguousarray(a["ctx_768"].transpose(0, 2, 1)),
        "weights": np.stack([a["L0_xattn_Wq"], pad(a["L0_xattn_Wk"]), pad(a["L0_xattn_Wv"]), a["L0_xattn_Wo"],
                             a["L0_ffn_Wq"].T, a["L0_ffn_Wk"].T, a["L0_ffn_Wv"].T, a["L0_ffn_Wp"].T]),
        "g_xattn": a["g_xattn"], "g_ffn": a["g_ffn"], "xattn_bo": a["L0_xattn_bo"],
        "bq": channels(a["L0_ffn_bq"]), "bk": channels(a["L0_ffn_bk"]), "bv": a["L0_ffn_bv"], "bp": a["L0_ffn_bp"],
        "wg": np.concatenate([a["L0_ffn_Wr"].T, np.zeros((DM, 1), np.float32), a["L0_ffn_Ws"].T], axis=1),
        "bg": np.concatenate([a["L0_ffn_br"], zero, a["L0_ffn_bs"]]),
        "temp": np.ascontiguousarray(a["L0_ffn_temperature"].reshape(NG, NG).T),
        "emb": channels(a["L0_ffn_query_embedding"].reshape(-1)),
    }
    nc = bacc.Bacc("TRN2", target_bir_lowering=False, num_devices=1, dynamic_dma_scratch_size=1024)
    feed, args = {}, []
    for name, arr in arrays.items():
        arr = np.ascontiguousarray(arr)
        feed[f"in_{name}"] = arr
        args.append(nc.dram_tensor(f"in_{name}", arr.shape, mybir.dt.from_np(arr.dtype), kind="ExternalInput").ap())
    out = nc.dram_tensor("out", [B, N, DM], F32, kind="ExternalOutput").ap()
    build(nc, *args, out)
    return run_bass_kernel_spmd(nc, [feed], core_ids=[0]).results[0]["out"]
```

```python
from contextlib import ExitStack

import concourse.bass as bass
from concourse import mybir

F32 = mybir.dt.float32
F32R = mybir.dt.float32r
ACT = mybir.ActivationFunctionType
ALU = mybir.AluOpType
AX = mybir.AxisListType

B, N, DM, DC = 8, 1024, 512, 384
P = 128
TT = N // P
HALF = N // 2
NG = DM // P
STEPS = 2 * TT
EPS = 1e-5
NE = 15
GC = 18
SH = 16
TOPK = 3


class Phase:

    def __init__(self, ffn):
        self.ffn = ffn
        self.D = 32 if ffn else 64
        self.G = P // self.D
        self.PAIRS = self.G // 2
        self.KC = (DM if ffn else DC) // P
        self.W = 4 if ffn else 0
        self.SCALE = float(self.D) ** -0.5
        self.SLOTS = 2 if ffn else 4
        self.MROW = 96 if ffn else 64
        self.NP = 10 if ffn else 8
        self.ADDER = ["dve", "pool", "pool", "pool"] if ffn else ["pool", "dve"]
        self.MX0 = 2
        self.SUM = 32 if ffn else 64

    def q_copies(self):
        return [("hi", 0, 0), ("lo", 32, 0), ("hi", 64, 0)] if self.ffn else [("hi", 0, 0), ("lo", 64, 0), ("hi", 0, 1)]

    def k_copies(self):
        return [("hi", 0, 1), ("hi", 32, 1), ("lo", 64, 1)] if self.ffn else [("hi", 0, 2), ("hi", 64, 2), ("lo", 0, 3)]

    def max_operands(self):
        return (0, 1, 96) if self.ffn else (0, 2, 128)

    def score_passes(self):
        return [(1, 0)] if self.ffn else [(2, 0), (3, 1)]

    def m_stack(self):
        return 0 if self.ffn else 1

    def one_stack(self):
        return 1 if self.ffn else 3



def maxima(ph, g):
    return [("mx", g, e, t, j) for e in range(ph.G) for t in range(TT) for j in range(2)]


def chunks(ph, kind):
    return ph.KC if kind == "pk" else NG


def projected(ph, g, kind):
    s = []
    for n in range(2):
        s += [(kind, g, n, c) for c in range(chunks(ph, kind))]
        if kind == "pk":
            s += [("pkl", g, n)]
        elif ph.ffn:
            s += [("ss", g, n), ("s2", g, n), ("s3", g, n)]
        else:
            s += [("pql", g, n)]
    return s


def normalised(ph):
    s = [] if ph.ffn else [("xl", 0), ("cx", 0), ("xl", 1), ("cx", 1)]
    for n in range(2):
        s += [("xl", 2 + n), ("ln", n), ("l2", n)]
        for k in range(NG):
            s += [("tr", n, k), ("trl", n, k)]
    return s


def spread(slots, items, first, last):
    for i, it in enumerate(items):
        slots[first + i * (last - first) // len(items)].append(it)


def schedule(ph, this, following):
    if not this:
        s = [("wl", 0)] + normalised(ph) + projected(ph, 0, "pq") + projected(ph, 0, "pk")
        return s + [("sd", 0), ("wl", 1)] + maxima(ph, 0) + [("nm", 0), ("mt", 0), ("ml", 0), ("md", 0)]
    s = [("wv", 0)]
    slots = [[] for _ in range(TT)]
    spread(slots, projected(ph, 1, "pq") + projected(ph, 1, "pk"), 0, TT - 1)
    for t in range(TT):
        s += slots[t] + [("vp", t)]
    s += [("wo", 0), ("sd", 1), ("wl", 2)]
    per = ph.G + 1
    tail = []
    s += [("S", 0, e) for e in range(ph.G)]
    for g in range(NG):
        slots = [[] for _ in range(per * STEPS)]
        if g + 1 < NG:
            spread(slots, maxima(ph, g + 1), ph.MX0 * per, (STEPS - 2) * per - 1)
            slots[(STEPS - 2) * per] += [("nm", g + 1), ("mt", g + 1), ("ml", g + 1), ("md", g + 1)]
        if g + 2 < NG:
            spread(slots, projected(ph, g + 2, "pq") + projected(ph, g + 2, "pk"), 5 * per, (STEPS - 1) * per)
            slots[-1] += [("wl", (g + 3) % NG)] if g + 3 < NG or following else []
        elif g == 2 and following:
            spread(slots, normalised(ph), 1 * per, (STEPS - 1) * per)
        elif g == 3 and following:
            spread(slots, projected(ph, 0, "pq") + projected(ph, 0, "pk"), 0, 6 * per)
            slots[6 * per] += [("sd", 0), ("wl", 1)]
            m = maxima(ph, 0)
            now = len(m) * 3 // 4
            spread(slots, m[:now], 8 * per, STEPS * per)
            tail = m[now:] + [("nm", 0), ("mt", 0), ("ml", 0), ("md", 0)]
        for st in range(STEPS):
            T = g * STEPS + st
            for e in range(ph.G):
                if T + 1 < NG * STEPS:
                    s += [("S", T + 1, e)]
                s += slots[st * per + e]
            h = T // TT - 1
            s += [("ad", T), ("PV", T)]
            behind = slots[st * per + ph.G]
            if T % TT == 0 and h >= 0:
                s += [("sm", h // 2, h % 2)] + behind[:1] + [("ev", h // 2, h % 2)] + behind[1:]
            else:
                s += behind
        if g + 2 < NG:
            s += [("sd", g + 2)]
    s += [("xr", 0)] + tail[:len(tail) // 2] + [("sm", NG - 1, 1), ("ev", NG - 1, 1)] + tail[len(tail) // 2:]
    if ph.ffn:
        for t in range(TT):
            s += [("hs", t, 0), ("gt", t)]
        s += [("gm", 0)]
    for t in range(TT):
        s += [("hs", t, 1), ("xb", t), ("op", t)]
    return s


class Order:

    def __init__(self, ph, items):
        self.items = items
        self.pos = {it: i for i, it in enumerate(items)}
        assert len(self.pos) == len(items)
        lower = {"tr": "trl", "pk": "pkl", "ss": "s2", "mt": "ml", "sm": "ev"}
        if not ph.ffn:
            lower["pq"] = "pql"
        by_act = ("pq",) if ph.ffn else ("vp",)
        self.bank, self.before, self.full, self.first, emptied = {}, {}, {}, {}, {}
        last, used = [None] * 3, [-3, -2, -1]
        for at, it in enumerate(items):
            kind = it[0]
            if kind not in ("tr", "pq", "pk", "ss", "vp", "mx", "mt", "sm", "gt", "op"):
                continue
            unit = self.unit(it)
            if unit not in self.bank:
                ring = {"mx": (0, 1), "sm": (0, 1), "mt": (0, 1), "vp": (0, 1), "op": (0, 1, 2)}.get(kind, (2,))
                b = min(ring, key=lambda x: used[x])
                self.bank[unit], self.before[unit], self.first[unit] = b, last[b], at
                last[b] = unit
            used[self.bank[unit]] = at
            if (kind in ("pq", "pk") and it[3] < chunks(ph, kind) - 1) or (kind == "gt" and it[1] < TT - 1):
                continue
            self.full[unit] = len(self.full) + 1
            emptied[("gm", 0) if kind == "gt" else (lower[kind],) + unit[1:] if kind in lower else it] = unit
        counts = {"act": 0, "dve": 0}
        self.drained = {}
        where = {}
        for at, it in enumerate(items):
            if it in emptied:
                engine = "act" if it[0] in by_act else "dve"
                counts[engine] += 1
                self.drained[emptied[it]] = (engine, counts[engine])
                where[emptied[it]] = at
        for unit, prior in self.before.items():
            assert prior is None or where[prior] < self.first[unit]

    @staticmethod
    def unit(it):
        return ("gt",) if it[0] == "gt" else it[:3] if it[0] in ("pq", "pk") else it

    def nth(self, it, by, same=lambda x: True):
        if it not in self.pos or self.pos[it] > self.pos[by]:
            return 0
        return [x for x in self.items if x[0] == it[0] and same(x)].index(it) + 1

    def so_far(self, kind, by, same=lambda x: True):
        return sum(1 for x in self.items[:self.pos[by]] if x[0] == kind and same(x))


def split_weights(nc, weights, w_split):
    with ExitStack() as ctx:
        sb = lambda name, shape, dt: ctx.enter_context(nc.sbuf_tensor(name, shape, dt))
        sem = lambda name: ctx.enter_context(nc.semaphore(name))
        raw = sb("w_raw", [P, NG, DM], F32)
        hi = sb("w_hi", [P, NG, DM], F32R)
        lo = sb("w_lo", [P, NG, DM], F32R)
        raw_in, hi_ok, lo_ok, out_ok = sem("w_raw_in"), sem("w_hi_ok"), sem("w_lo_ok"), sem("w_out_ok")
        with nc.Fori(0, 8) as w:
            with nc.Block() as block:

                @block.sync
                def _(sp):
                    sp.dma_start(raw[:], weights[bass.ds(w, 1)].rearrange("a (k p) c -> p (a k) c", p=P)).then_inc(raw_in, 16)
                    sp.wait_ge(lo_ok, 1)
                    for part, src in enumerate((hi, lo)):
                        for g in range(NG):
                            sp.dma_start(w_split[bass.ds(w, 1), part, g].rearrange("a p k c -> p (a k) c"),
                                         src[:, :, g * P:(g + 1) * P].bitcast(F32)).then_inc(out_ok, 16)
                    sp.wait_ge(out_ok, 2 * NG * 16)

                @block.scalar
                def _(act):
                    act.wait_ge(raw_in, 16)
                    act.activation(hi[:], raw[:], ACT.Copy).then_inc(hi_ok, 1)

                @block.vector
                def _(dve):
                    dve.wait_ge(raw_in, 16)
                    dve.wait_ge(hi_ok, 1)
                    dve.tensor_tensor(lo[:], raw[:], hi[:].bitcast(F32), ALU.subtract).then_inc(lo_ok, 1)

            for s in (raw_in, hi_ok, lo_ok, out_ok):
                nc.sync.sem_clear(s)
            nc.all_engine_barrier()


def attention_phase(nc, ph, x_in, ctxT, w_split, bias_row, gate_scalar, x_out, small):
    ffn, D, G, KC = ph.ffn, ph.D, ph.G, ph.KC
    NCOPY = 6 * 16
    HALVES = 2 * NG
    pre = "f_" if ffn else "x_"
    with ExitStack() as ctx:
        sb = lambda name, shape, dt=F32: ctx.enter_context(nc.sbuf_tensor(pre + name, shape, dt))
        made = []

        def sem(name, cleared=True):
            s = ctx.enter_context(nc.semaphore(pre + name))
            if cleared:
                made.append(s)
            return s

        xs = sb("xs", [P, TT // 2, DM])
        raw = xs[:].rearrange("p (t a) d -> p t (a d)", a=2)
        xT_hi = sb("xT_hi", [P, NG, N], F32R)
        xT_lo = sb("xT_lo", [P, NG, N], F32R)
        if ffn:
            kv_hi, kv_lo = xT_hi, xT_lo
        else:
            kv_hi = sb("kv_hi", [P, KC, N], F32R)
            kv_lo = sb("kv_lo", [P, KC, N], F32R)
        wqk = sb("wqk", [P, 2, 2, NG, P], F32R)
        wvo = sb("wvo", [P, 2, NG, NG, P], F32R)
        stack = sb("stack", [P, 2, G * ph.SLOTS, N], F32R)
        cq = {h: sb(f"cq_{h}", [P, N], F32R) for h in ("hi", "lo")}
        ck = {h: sb(f"ck_{h}", [P, N], F32R) for h in ("hi", "lo")}
        vh = sb("vh", [P, HALVES + 1, HALF])
        v = vh[:, 1:HALVES + 1, :].rearrange("p (g a) c -> p g (a c)", a=2)
        probs = sb("probs", [P, ph.NP, HALF])
        NACC = 2 * G
        added = sb("added", [P, NACC, HALF])
        rn = sb("rn", [P, HALF])
        mx = sb("mx", [P, G * TT, 2])
        nm = sb("nm", [P, G * TT])
        mrow = sb("mrow", [G * TT, P], F32R)
        ident = sb("ident", [P, P])
        ones = sb("ones", [P, ph.SUM])
        bo = sb("bo", [P, DM])
        tg = sb("tg", [P, 1])
        st = sb("st", [P, TT, 6])
        mv = sb("mv", [P, TT, 2])
        rs = sb("rs", [P, 3, TT])
        if ffn:
            qb = sb("qb", [P, 2, HALF])
            sq = sb("sq", [P, 2, HALF])
            qy = sb("qy", [P, 2, HALF])
            blk = sb("blk", [P, P])
            bq, bk = sb("bq", [P, NG]), sb("bk", [P, NG])
            emb, tau, et = sb("emb", [P, NG]), sb("tau", [P, NG]), sb("et", [P, NG])
            tmp = sb("tmp", [P, 3, NG])
            bv = sb("bv", [P, DM])
            wg = sb("wg", [P, NG, GC])
            wg_hi, wg_lo = sb("wg_hi", [P, NG, GC], F32R), sb("wg_lo", [P, NG, GC], F32R)
            bg = sb("bg", [P, GC])
            lg = sb("lg", [P, TT, GC])
            eg = sb("eg", [P, TT, GC])
            gm = sb("gm", [P, TT, 2])
            top = sb("top", [P, TT, 8])
            g1 = sb("g1", [P, 4, TT])
            sw = sb("sw", [P, TT, 2])
            sc = sb("sc", [P, TT])
        acc = ctx.enter_context(nc.psum_tensor(pre + "acc", [P, 2, HALF], F32))
        scores = ctx.enter_context(nc.psum_tensor(pre + "scores", [P, 3, HALF], F32))
        aux = ctx.enter_context(nc.psum_tensor(pre + "aux", [P, 3, HALF], F32))

        def split_slot(t):
            c = cq if t % 4 < 2 else ck
            return [c[half][:, t % 2 * HALF:(t % 2 + 1) * HALF].rearrange("p (g c) -> p g c", g=NG) for half in ("hi", "lo")]

        def splits(t, r):
            return t + 1 + (TT * r if ffn else 0)

        def outputs(t):
            first = t // (TT // 2)
            pieces = vh[:, 0:HALVES, :].rearrange("p (g n) c -> p g n c", n=2)
            return pieces[:, :, first, t % (TT // 2) * P:(t % (TT // 2) + 1) * P]

        def exp_buffer(T, e):
            if T % TT == 0:
                return added[:, (T // TT % 2) * G + e, :], None
            m = (T - T // TT - 1) * G + e
            prior = None
            if m >= ph.NP:
                s, head = divmod(m - ph.NP, G)
                prior = (s + s // (TT - 1) + 1, head)
            return probs[:, m % ph.NP, :], prior

        def adds(T, e):
            mine = [h for h in range(G) if ph.ADDER[h] == ph.ADDER[e]]
            return (T - T // TT - 1) * len(mine) + mine.index(e) + 1

        c_in, c_ms, c_act, c_dve = (sem(n, False) for n in ("c_in", "c_ms", "c_act", "c_dve"))
        c_abs = sem("c_abs", False)
        n_const = 2 + (2 + 3 + 1 + G if ffn else 0)
        with nc.Block() as block:

            @block.sync
            def _(sp):
                sp.dma_start(tg[:], gate_scalar.partition_broadcast(P)).then_inc(c_in, 16)
                sp.dma_start(bo[:], bias_row.partition_broadcast(P)).then_inc(c_in, 16)
                if ffn:
                    sp.dma_start(bv[:], small["bv"].partition_broadcast(P)).then_inc(c_in, 16)
                    sp.dma_start(bg[:], small["bg"].partition_broadcast(P)).then_inc(c_in, 16)
                    for dst, name in ((bq, "bq"), (bk, "bk"), (emb, "emb")):
                        sp.dma_start(dst[:], small[name]).then_inc(c_in, 16)
                    sp.dma_start(wg[:], small["wg"].rearrange("(k p) c -> p k c", p=P)).then_inc(c_in, 16)
                    for e in range(G):
                        sp.dma_start(tau[e * D:(e + 1) * D, :], small["temp"][e].partition_broadcast(D)).then_inc(c_in, 16)

            @block.gpsimd
            def _(pool):
                pool.memset(ident[:], 0.0).then_inc(c_ms, 1)
                pool.memset(ones[:], 1.0).then_inc(c_ms, 1)
                pool.wait_ge(c_ms, 2)
                pool.affine_select(out=ident[:], in_=ident[:], compare_op=ALU.not_equal, fill=1.0, base=0,
                                   pattern=[[-1, P]], channel_multiplier=1).then_inc(c_ms, 1)

            @block.vector
            def _(dve):
                done = [0]

                def link(ins):
                    done[0] += 1
                    ins.then_inc(c_dve, 1)
                    dve.wait_ge(c_dve, done[0])

                for par in range(2):
                    for e in range(G):
                        for slot in (ph.m_stack(), ph.one_stack()):
                            link(dve.memset(stack[ph.MROW:P, par, e * ph.SLOTS + slot, :].bitcast(F32), 0.0))
                        link(dve.memset(stack[ph.MROW:ph.MROW + 1, par, e * ph.SLOTS + ph.one_stack(), :].bitcast(F32), 1.0))
                if ffn:
                    link(dve.memset(blk[:], 0.0))
                    for e in range(G):
                        link(dve.memset(blk[e * D:(e + 1) * D, e * D:(e + 1) * D], 1.0))
                dve.wait_ge(c_act, 1)
                link(dve.tensor_scalar(bo[:], bo[:], tg[:, 0:1], None, ALU.mult))
                if ffn:
                    link(dve.tensor_scalar(tmp[:, 0], tau[:], -1.0, None, ALU.mult))
                    dve.tensor_tensor(tmp[:, 0], tau[:], tmp[:, 0], ALU.min).then_inc(c_abs, 1)
                    dve.wait_ge(c_act, 3)
                    link(dve.tensor_scalar(tau[:], tau[:], 0.0, None, ALU.max))
                    link(dve.tensor_tensor(tau[:], tau[:], tmp[:, 2], ALU.add))
                    link(dve.tensor_tensor(et[:], emb[:], tau[:], ALU.mult))
                    link(dve.tensor_copy(wg_hi[:], wg[:]))
                    link(dve.tensor_tensor(wg_lo[:], wg[:], wg_hi[:].bitcast(F32), ALU.subtract))

            @block.scalar
            def _(act):
                act.wait_ge(c_in, 16 * n_const)
                act.activation(tg[:], tg[:], ACT.Tanh).then_inc(c_act, 1)
                act.preload_act_table_set("natural_log_exp_and_others")
                if ffn:
                    act.wait_ge(c_abs, 1)
                    act.activation(tmp[:, 1], tmp[:, 0], ACT.Exp).then_inc(c_act, 1)
                    act.wait_ge(c_act, 2)
                    act.activation(tmp[:, 2], tmp[:, 1], ACT.Ln, bias=1.0).then_inc(c_act, 1)

        xs_loaded = [sem(f"xs_loaded{i}") for i in range(4)]
        x_again = [sem(f"x_again{i}") for i in range(TT)]
        stored = [sem(f"stored{i}") for i in range(TT)]
        w_loaded, wv_loaded, wo_loaded = sem("w_loaded"), sem("wv_loaded"), sem("wo_loaded")
        stacked = [[sem(f"stacked{i}_{e}") for e in range(G)] for i in range(2)]
        m_stacked = [sem(f"m_stacked{i}") for i in range(2)]
        ctx_hi_ok, ctx_lo_ok = sem("ctx_hi_ok"), sem("ctx_lo_ok")
        normed = sem("normed")
        rstd_in, rstd_ok = sem("rstd_in"), sem("rstd_ok")
        aux_full = sem("aux_full")
        emptied = {"act": sem("emptied_by_act"), "dve": sem("emptied_by_dve")}
        hi_ok = sem("hi_ok")
        sq_ok, y_ok, qn_ok, qs_ok, qlo_ok = (sem(n) for n in ("sq_ok", "y_ok", "qn_ok", "qs_ok", "qlo_ok"))
        nm_ok = sem("nm_ok")
        scored, probs_ok, weighed = sem("scored"), sem("probs_ok"), sem("weighed")
        added_ok = {"dve": sem("added_by_dve"), "pool": sem("added_by_pool")}
        rinv_ok, out_ok = sem("rinv_ok"), sem("out_ok")
        h_hi_ok, h_lo_ok, biased = sem("h_hi_ok"), sem("h_lo_ok"), sem("biased")
        gated = sem("gated")
        gates_in, gates_exp = sem("gates_in"), sem("gates_exp")
        act_chain, dve_chain = sem("act_chain"), sem("dve_chain")

        def turn(sched, x_this, out_this, x_next, ctx_next):
            o = Order(ph, sched)
            MAKES_HI = ("tr", "pk") if ffn else ("tr", "pk", "pq")
            hi_units = [u for u in o.full if u[0] in MAKES_HI]
            q_units = [u for u in o.full if u[0] == "pq"]
            ends = lambda it: it[0] not in ("pq", "pk") or it[3] == chunks(ph, it[0]) - 1
            mine = lambda g: lambda x: x[1] % 2 == g % 2

            def wait_full(eng, unit):
                eng.wait_ge(aux_full, o.full[unit])

            def wait_emptied(eng, unit):
                who, n = o.drained[unit]
                eng.wait_ge(emptied[who], n)

            def wait_stacked(eng, g, e, by):
                n = o.nth(("sd", g), by, mine(g))
                if n:
                    eng.wait_ge(stacked[g % 2][e], NCOPY * n)

            def wait_copies_left(eng, by):
                before = [x for x in sched[:o.pos[by]] if x[0] == "sd"]
                if before:
                    for e in range(G):
                        wait_stacked(eng, before[-1][1], e, by)

            with nc.Block() as block:

                @block.sync
                def _(sp):
                    for it in sched:
                        kind, g = it[0], it[1]
                        if kind == "xl":
                            if g < 2:
                                if g:
                                    sp.wait_ge(ctx_lo_ok, 1)
                                tiles = slice(2 * g, min(2 * g + 2, KC))
                                sp.dma_start(raw[:, 0:tiles.stop - tiles.start, :],
                                             ctx_next.rearrange("a (k p) n -> p (a k) n", p=P)[:, tiles, :]).then_inc(xs_loaded[g], 16)
                            else:
                                if g == 3:
                                    wait_full(sp, ("tr", 0, NG - 1))
                                elif not ffn:
                                    sp.wait_ge(ctx_lo_ok, KC)
                                sp.dma_start(xs[:], x_next.rearrange("a (t p) d -> p (a t) d", p=P)[:, (g - 2) * TT // 2:(g - 1) * TT // 2, :]).then_inc(xs_loaded[g], 16)
                        elif kind == "wl":
                            before = [x for x in sched[:o.pos[it]] if x[0] == "pk"]
                            if before:
                                wait_full(sp, before[-1][:3])
                            for what in range(2):
                                for part in range(2):
                                    sp.dma_start(wqk[:, what, part].bitcast(F32), w_split[ph.W + what, part, g]).then_inc(w_loaded, 16)
                        elif kind in ("wv", "wo"):
                            if kind == "wo":
                                wait_full(sp, ("vp", TT - 1))
                            w, done = (ph.W + 2, wv_loaded) if kind == "wv" else (ph.W + 3, wo_loaded)
                            for part in range(2):
                                sp.dma_start(wvo[:, part].bitcast(F32), w_split[w, part].rearrange("g p k c -> p k g c")).then_inc(done, 16)
                        elif kind == "sd":
                            steps = [x[1] for x in sched[:o.pos[it]] if x[0] == "S" and x[1] // STEPS % 2 == g % 2]
                            if steps:
                                sp.wait_ge(scored, (max(steps) + 1) * G)
                            if ffn:
                                sp.wait_ge(qlo_ok, q_units.index(("pq", g, 1)) + 1)
                            else:
                                wait_emptied(sp, ("pq", g, 1))
                            wait_emptied(sp, ("pk", g, 1))
                            for e in range(G):
                                for src, copies in ((cq, ph.q_copies()), (ck, ph.k_copies())):
                                    for half, row, slot in copies:
                                        sp.dma_start(stack[row:row + D, g % 2, e * ph.SLOTS + slot, :].bitcast(F32),
                                                     src[half][e * D:(e + 1) * D, :].bitcast(F32)).then_inc(stacked[g % 2][e], 16)
                        elif kind == "md":
                            wait_emptied(sp, ("mt", g))
                            for e in range(G):
                                dst = stack[ph.MROW:ph.MROW + 1, g % 2, e * ph.SLOTS + ph.m_stack(), :]
                                sp.dma_start(dst.rearrange("o (t q) -> o t q", q=P).bitcast(F32),
                                             mrow[e * TT:(e + 1) * TT, :].bitcast(F32)).then_inc(m_stacked[g % 2], 16)
                        elif kind == "xr":
                            if ("tr", 1, NG - 1) in o.full:
                                wait_full(sp, ("tr", 1, NG - 1))
                            for t in range(TT // 2):
                                sp.dma_start(xs[:, t, :], x_this.rearrange("a (t p) d -> p (a t) d", p=P)[:, t, :]).then_inc(x_again[t], 16)
                        elif kind == "op":
                            t = g
                            wait_emptied(sp, it)
                            sp.dma_start(out_this.rearrange("a (t p) d -> p (a t) d", p=P)[:, t, :], xs[:, t % (TT // 2), :]).then_inc(stored[t], 16)
                            if t < TT // 2:
                                sp.wait_ge(stored[t], 16)
                                sp.dma_start(xs[:, t, :], x_this.rearrange("a (t p) d -> p (a t) d", p=P)[:, t + TT // 2, :]).then_inc(x_again[t + TT // 2], 16)
                    sp.wait_ge(w_loaded, 64 * sum(x[0] == "wl" for x in sched))
                    for i in range(2):
                        rows = sum(x[0] == "md" and x[1] % 2 == i for x in sched)
                        if rows:
                            sp.wait_ge(m_stacked[i], G * 16 * rows)
                    if x_this is not None:
                        for t in range(TT // 2, TT):
                            sp.wait_ge(stored[t], 16)

                def add(eng, name, T):
                    for e in range(G):
                        if ph.ADDER[e] != name:
                            continue
                        onto, _ = exp_buffer(T - T % TT, e)
                        eng.wait_ge(probs_ok, T * G + e + 1)
                        if T % TT == 1:
                            eng.wait_ge(weighed, T)
                        else:
                            eng.wait_ge(added_ok[name], adds(T - 1, e))
                        eng.tensor_tensor(onto, onto, exp_buffer(T, e)[0], ALU.add).then_inc(added_ok[name], 1)

                @block.gpsimd
                def _(pool):
                    for it in sched:
                        kind = it[0]
                        if kind == "cx":
                            for k in range(2 * it[1], min(2 * it[1] + 2, KC)):
                                pool.wait_ge(ctx_hi_ok, k + 1)
                                pool.tensor_tensor(kv_lo[:, k, :], raw[:, k % 2, :], kv_hi[:, k, :].bitcast(F32), ALU.subtract).then_inc(ctx_lo_ok, 1)
                        elif kind == "s3":
                            _, g, n = it
                            pool.wait_ge(qs_ok, 2 * q_units.index(("pq", g, n)) + 2)
                            q = slice(n * HALF, (n + 1) * HALF)
                            pool.tensor_tensor(cq["lo"][:, q], qy[:, n], cq["hi"][:, q].bitcast(F32), ALU.subtract).then_inc(qlo_ok, 1)
                        elif kind == "ad" and it[1] % TT:
                            add(pool, "pool", it[1])
                        elif kind == "hs":
                            t = it[1]
                            hi, lo = split_slot(t)
                            pool.wait_ge(h_hi_ok, splits(t, it[2]))
                            pool.tensor_tensor(lo, outputs(t), hi.bitcast(F32), ALU.subtract).then_inc(h_lo_ok, 1)
                        elif kind == "xb":
                            t = it[1]
                            pool.wait_ge(x_again[t], 16)
                            pool.tensor_tensor(xs[:, t % (TT // 2), :], xs[:, t % (TT // 2), :], bo[:], ALU.add).then_inc(biased, 1)

                @block.tensor
                def _(pe):
                    def bank(it):
                        unit = o.unit(it)
                        if o.before[unit] and o.first[unit] == o.pos[it]:
                            wait_emptied(pe, o.before[unit])
                        return aux[:, o.bank[unit], :]

                    def product(out, lhs, rhs, tiles, whole):
                        for k in tiles:
                            for i, (a, c) in enumerate(((0, 0), (0, 1), (1, 0))):
                                ins = pe.matmul(out, lhs(a, k), rhs(c, k), start=k == 0 and i == 0, stop=k == whole - 1 and i == 2)
                        return ins

                    xT, kvT = (xT_hi, xT_lo), (kv_hi, kv_lo)

                    def wait_source(keys):
                        if keys and not ffn:
                            if made_context:
                                pe.wait_ge(ctx_lo_ok, KC)
                        elif made_x:
                            wait_emptied(pe, ("tr", 1, NG - 1))

                    made_context = made_x = False
                    for it in sched:
                        kind = it[0]
                        if kind == "cx":
                            made_context = it[1] == 1
                        elif kind == "tr":
                            _, n, k = it
                            made_x = (n, k) == (1, NG - 1)
                            pe.wait_ge(normed, n + 1)
                            out = bank(it)
                            for i in range(TT // 2):
                                ins = pe.transpose(out[:, i * P:(i + 1) * P], xs[:, i, k * P:(k + 1) * P], ident[:])
                            ins.then_inc(aux_full, 1)
                        elif kind in ("pq", "pk"):
                            _, g, n, c0 = it
                            what = int(kind == "pk")
                            if c0 == 0:
                                loads = o.nth(("wl", g), it)
                                if loads:
                                    pe.wait_ge(w_loaded, 64 * loads)
                                wait_source(what)
                            src = kvT if what else xT
                            q = slice(n * HALF, (n + 1) * HALF)
                            ins = product(bank(it), lambda a, k: wqk[:, what, a, k, :], lambda c, k: src[c][:, k, q], [c0], chunks(ph, kind))
                            if ends(it):
                                ins.then_inc(aux_full, 1)
                        elif kind == "ss":
                            _, g, n = it
                            out = bank(it)
                            pe.wait_ge(sq_ok, q_units.index(("pq", g, n)) + 1)
                            pe.matmul(out, blk[:], sq[:, n], start=True, stop=True).then_inc(aux_full, 1)
                        elif kind == "vp":
                            t = it[1]
                            pe.wait_ge(wv_loaded, 32)
                            r = slice(t * P, (t + 1) * P)
                            product(bank(it), lambda a, k: kvT[a][:, k, r], lambda c, k: wvo[:, c, k].rearrange("p g c -> p (g c)"),
                                    range(KC), KC).then_inc(aux_full, 1)
                        elif kind == "mx":
                            _, g, e, t, j = it
                            qs, ks, rows = ph.max_operands()
                            out = bank(it)
                            wait_stacked(pe, g, e, it)
                            pe.matmul(out, stack[0:rows, g % 2, e * ph.SLOTS + qs, t * P:(t + 1) * P],
                                      stack[0:rows, g % 2, e * ph.SLOTS + ks, j * HALF:(j + 1) * HALF],
                                      start=True, stop=True).then_inc(aux_full, 1)
                        elif kind == "mt":
                            g = it[1]
                            out = bank(it)
                            pe.wait_ge(nm_ok, o.nth(("nm", g), it))
                            pe.transpose(out[0:G * TT, 0:P], nm[:], ident[:]).then_inc(aux_full, 1)
                        elif kind == "S":
                            _, T, e = it
                            g, s = divmod(T, STEPS)
                            n, jt = divmod(s, TT)
                            if s == 0 and e == 0 and o.nth(("md", g), it, mine(g)):
                                pe.wait_ge(m_stacked[g % 2], G * 16 * o.nth(("md", g), it, mine(g)))
                            u = T * G + e
                            if u >= 3:
                                pe.wait_ge(probs_ok, u - 2)
                            passes = ph.score_passes()
                            for a, (ks, qs) in enumerate(passes):
                                ins = pe.matmul(scores[:, u % 3, :], stack[:, g % 2, e * ph.SLOTS + ks, jt * P:(jt + 1) * P],
                                                stack[:, g % 2, e * ph.SLOTS + qs, n * HALF:(n + 1) * HALF],
                                                start=a == 0, stop=a == len(passes) - 1)
                            ins.then_inc(scored, 1)
                        elif kind == "PV":
                            T = it[1]
                            h, jt = divmod(T, TT)
                            g = h // 2
                            pe.wait_ge(probs_ok, (T + 1) * G)
                            if T == 0:
                                wait_emptied(pe, ("vp", TT - 1))
                            if jt == 0 and h >= 2:
                                pe.wait_ge(out_ok, h - 1)
                            for e in range(G):
                                ins = pe.matmul(acc[e * D:(e + 1) * D, h % 2, :], v[:, g, jt * P + e * D:jt * P + (e + 1) * D],
                                                exp_buffer(T, e)[0], start=jt == 0, stop=jt == TT - 1)
                            ins.then_inc(weighed, 1)
                        elif kind == "sm":
                            _, g, n = it
                            h = 2 * g + n
                            out = bank(it)
                            for name in ("dve", "pool"):
                                top_head = max(e for e in range(G) if ph.ADDER[e] == name)
                                pe.wait_ge(added_ok[name], adds(h * TT + TT - 1, top_head))
                            for e in range(G):
                                ins = pe.matmul(out[e * D:(e + 1) * D, :], ones[:], added[:, h % 2 * G + e, :], start=True, stop=True)
                            ins.then_inc(aux_full, 1)
                        elif kind == "gt":
                            t = it[1]
                            out = bank(it)
                            hi_lo = split_slot(t)
                            pe.wait_ge(h_lo_ok, splits(t, 0))
                            ins = product(out[:, t * GC:(t + 1) * GC], lambda a, k: hi_lo[a][:, k, :], lambda c, k: (wg_hi, wg_lo)[c][:, k, :], range(NG), NG)
                            ins.then_inc(gated if t < TT - 1 else aux_full, 1)
                        elif kind == "op":
                            t = it[1]
                            out = bank(it)
                            hi_lo = split_slot(t)
                            pe.wait_ge(wo_loaded, 32)
                            pe.wait_ge(h_lo_ok, splits(t, 1))
                            product(out, lambda a, k: hi_lo[a][:, k, :], lambda c, k: wvo[:, c, k].rearrange("p g c -> p (g c)"),
                                    range(NG), NG).then_inc(aux_full, 1)

                @block.scalar
                def _(act):
                    chain = [0]

                    def link(ins):
                        chain[0] += 1
                        ins.then_inc(act_chain, 1)
                        act.wait_ge(act_chain, chain[0])

                    def full(unit):
                        wait_full(act, unit)
                        return aux[:, o.bank[unit], :]

                    for it in sched:
                        kind = it[0]
                        if kind == "cx":
                            act.wait_ge(xs_loaded[it[1]], 16)
                            if it[1] == 0 and ("pk", NG - 1, 1) in o.full:
                                wait_full(act, ("pk", NG - 1, 1))
                            for k in range(2 * it[1], min(2 * it[1] + 2, KC)):
                                act.activation(kv_hi[:, k, :], raw[:, k % 2, :], ACT.Copy).then_inc(ctx_hi_ok, 1)
                        elif kind == "ln":
                            n = it[1]
                            r = slice(n * TT // 2, (n + 1) * TT // 2)
                            act.wait_ge(rstd_in, n + 1)
                            link(act.activation(rs[:, 1, r], rs[:, 0, r], ACT.Ln))
                            act.activation(rs[:, 1, r], rs[:, 1, r], ACT.Exp, scale=-0.5).then_inc(rstd_ok, 1)
                        elif kind == "tr":
                            _, n, k = it
                            act.activation(xT_hi[:, k, n * HALF:(n + 1) * HALF], full(it), ACT.Copy).then_inc(hi_ok, 1)
                        elif kind in MAKES_HI and ends(it):
                            _, g, n, _ = it
                            if n == 0:
                                wait_copies_left(act, it)
                            src = full(it[:3])
                            dst = (cq if kind == "pq" else ck)["hi"][:, n * HALF:(n + 1) * HALF]
                            if ffn:
                                act.activation(dst, src, ACT.Identity, bias=bk[:, g:g + 1]).then_inc(hi_ok, 1)
                            else:
                                act.activation(dst, src, ACT.Copy).then_inc(hi_ok, 1)
                        elif kind == "pq" and ends(it):
                            _, g, n, _ = it
                            src = full(it[:3])
                            i = q_units.index(it[:3])
                            if i >= 2:
                                act.wait_ge(qs_ok, 2 * (i - 2) + 1)
                            act.activation(sq[:, n], src, ACT.Square, bias=bq[:, g:g + 1]).then_inc(sq_ok, 1)
                            act.activation(qb[:, n], src, ACT.Identity, bias=bq[:, g:g + 1]).then_inc(emptied["act"], 1)
                        elif kind == "ss":
                            _, g, n = it
                            i = q_units.index(("pq", g, n))
                            if i >= 2:
                                act.wait_ge(qlo_ok, i - 1)
                            link(act.activation(qy[:, n], full(it), ACT.Ln))
                            link(act.activation(qy[:, n], qy[:, n], ACT.Exp, scale=-0.5))
                            act.activation(sq[:, n], qy[:, n], ACT.Square).then_inc(y_ok, 1)
                        elif kind == "s3":
                            _, g, n = it
                            i = q_units.index(("pq", g, n))
                            act.wait_ge(qn_ok, i + 1)
                            act.activation(qy[:, n], qb[:, n], ACT.Identity, scale=tau[:, g:g + 1], bias=et[:, g:g + 1]).then_inc(qs_ok, 1)
                            act.wait_ge(qs_ok, 2 * i + 1)
                            if n == 0:
                                wait_copies_left(act, it)
                            act.activation(cq["hi"][:, n * HALF:(n + 1) * HALF], qy[:, n], ACT.Copy).then_inc(qs_ok, 1)
                        elif kind == "vp" and not ffn:
                            t = it[1]
                            src = full(it)
                            act.activation(v[:, :, t * P:(t + 1) * P], src.rearrange("p (g c) -> p g c", g=NG), ACT.Copy).then_inc(emptied["act"], 1)
                        elif kind == "S":
                            _, T, e = it
                            u = T * G + e
                            dst, prior = exp_buffer(T, e)
                            h = T // TT
                            act.wait_ge(scored, u + 1)
                            if prior:
                                s, head = prior
                                act.wait_ge(weighed, s + 1)
                                act.wait_ge(added_ok[ph.ADDER[head]], adds(s, head))
                            if T % TT == 0 and h >= 2 and e == 0:
                                wait_full(act, ("sm", h // 2 - 1, h % 2))
                            act.activation(dst, scores[:, u % 3, :], ACT.Exp, scale=ph.SCALE).then_inc(probs_ok, 1)
                        elif kind == "sm":
                            _, g, n = it
                            h = 2 * g + n
                            src = full(it)
                            if h:
                                act.wait_ge(out_ok, h)
                            link(act.activation(rn[:], src, ACT.Ln))
                            act.activation(rn[:], rn[:], ACT.Exp, scale=-1.0).then_inc(rinv_ok, 1)
                        elif kind == "hs":
                            t = it[1]
                            act.wait_ge(out_ok, HALVES - 1 if t < TT // 2 else HALVES)
                            i = t + TT * it[2]
                            if i == 0 or (i == TT and not ffn):
                                wait_copies_left(act, it)
                            elif i >= TT + 4:
                                wait_full(act, ("op", t - 4))
                            elif 4 <= i < TT + 4 and ffn:
                                if i - 4 < TT - 1:
                                    act.wait_ge(gated, i - 3)
                                else:
                                    wait_full(act, ("gt",))
                            act.activation(split_slot(t)[0], outputs(t), ACT.Copy).then_inc(h_hi_ok, 1)
                        elif kind == "gm":
                            act.wait_ge(gates_in, 1)
                            act.activation(eg[:], lg[:], ACT.Exp).then_inc(gates_exp, 1)

                @block.vector
                def _(dve):
                    chain = [0]

                    def link(ins):
                        chain[0] += 1
                        ins.then_inc(dve_chain, 1)
                        dve.wait_ge(dve_chain, chain[0])

                    def full(unit):
                        wait_full(dve, unit)
                        return aux[:, o.bank[unit], :]

                    def newton(y, x, y2, out):
                        link(dve.scalar_tensor_tensor(y2, y2, -0.5, x, ALU.mult, ALU.mult))
                        return dve.scalar_tensor_tensor(out, y2, 1.5, y, ALU.add, ALU.mult)

                    for it in sched:
                        kind = it[0]
                        if kind in ("ln", "l2"):
                            n = it[1]
                            tiles = range(TT // 2)
                            r = slice(n * TT // 2, (n + 1) * TT // 2)
                            if kind == "ln":
                                dve.wait_ge(xs_loaded[2 + n], 16)
                                for t in tiles:
                                    ins = dve.bn_stats(st[:, r.start + t, :], xs[:, t, :])
                                link(ins)
                                for t in tiles:
                                    ins = dve.bn_aggr(mv[:, r.start + t, :], st[:, r.start + t, :])
                                link(ins)
                                dve.tensor_scalar(rs[:, 0, r], mv[:, r, 1], EPS, None, ALU.add).then_inc(rstd_in, 1)
                                continue
                            dve.wait_ge(rstd_in, n + 1)
                            dve.wait_ge(rstd_ok, n + 1)
                            link(dve.tensor_tensor(rs[:, 2, r], rs[:, 1, r], rs[:, 1, r], ALU.mult))
                            link(newton(rs[:, 1, r], rs[:, 0, r], rs[:, 2, r], rs[:, 1, r]))
                            for t in tiles:
                                i = r.start + t
                                ins = dve.tensor_scalar(xs[:, t, :], xs[:, t, :], mv[:, i, 0:1], rs[:, 1, i:i + 1], ALU.subtract, ALU.mult)
                            ins.then_inc(normed, 1)
                        elif kind == "trl":
                            _, n, k = it
                            unit = ("tr", n, k)
                            src = full(unit)
                            q = slice(n * HALF, (n + 1) * HALF)
                            dve.wait_ge(hi_ok, hi_units.index(unit) + 1)
                            dve.tensor_tensor(xT_lo[:, k, q], src, xT_hi[:, k, q].bitcast(F32), ALU.subtract).then_inc(emptied["dve"], 1)
                        elif kind in ("pkl", "pql"):
                            _, g, n = it
                            unit = (kind[:2], g, n)
                            src = full(unit)
                            q = slice(n * HALF, (n + 1) * HALF)
                            c = cq if kind == "pql" else ck
                            dve.wait_ge(hi_ok, hi_units.index(unit) + 1)
                            if ffn:
                                ins = dve.scalar_tensor_tensor(c["lo"][:, q], src, bk[:, g:g + 1], c["hi"][:, q].bitcast(F32), ALU.add, ALU.subtract)
                            else:
                                ins = dve.tensor_tensor(c["lo"][:, q], src, c["hi"][:, q].bitcast(F32), ALU.subtract)
                            ins.then_inc(emptied["dve"], 1)
                        elif kind == "s2":
                            _, g, n = it
                            unit = ("ss", g, n)
                            i = q_units.index(("pq", g, n))
                            src = full(unit)
                            dve.wait_ge(y_ok, i + 1)
                            wait_emptied(dve, ("pq", g, n))
                            dve.scalar_tensor_tensor(sq[:, n], sq[:, n], -0.5, src, ALU.mult, ALU.mult).then_inc(emptied["dve"], 1)
                            wait_emptied(dve, unit)
                            link(dve.scalar_tensor_tensor(qy[:, n], sq[:, n], 1.5, qy[:, n], ALU.add, ALU.mult))
                            dve.tensor_tensor(qb[:, n], qb[:, n], qy[:, n], ALU.mult).then_inc(qn_ok, 1)
                        elif kind == "vp" and ffn:
                            t = it[1]
                            src = full(it)
                            dve.tensor_tensor(v[:, :, t * P:(t + 1) * P], src.rearrange("p (g c) -> p g c", g=NG),
                                              bv[:].rearrange("p (g c) -> p g c", g=NG), ALU.add).then_inc(emptied["dve"], 1)
                        elif kind == "mx":
                            _, g, e, t, j = it
                            src = full(it)
                            dve.tensor_reduce(mx[:, e * TT + t, j:j + 1], src, axis=AX.X, op=ALU.max).then_inc(emptied["dve"], 1)
                        elif kind == "nm":
                            g = it[1]
                            wait_emptied(dve, ("mx", g, G - 1, TT - 1, 1))
                            dve.tensor_reduce(nm[:], mx[:], axis=AX.X, op=ALU.max, negate=True).then_inc(nm_ok, 1)
                        elif kind == "ml":
                            g = it[1]
                            src = full(("mt", g))
                            before = [x[1] for x in sched[:o.pos[it]] if x[0] == "md"]
                            if before:
                                dve.wait_ge(m_stacked[before[-1] % 2], G * 16 * o.nth(("md", before[-1]), it, mine(before[-1])))
                            dve.tensor_copy(mrow[:], src[0:G * TT, 0:P]).then_inc(emptied["dve"], 1)
                        elif kind == "ad" and it[1] % TT:
                            add(dve, "dve", it[1])
                        elif kind == "ev":
                            _, g, n = it
                            h = 2 * g + n
                            src = full(("sm", g, n))
                            dve.wait_ge(rinv_ok, h + 1)
                            dve.scalar_tensor_tensor(vh[:, h, :], src, -1.0, rn[:], ALU.mult, ALU.mult).then_inc(emptied["dve"], 1)
                            wait_emptied(dve, ("sm", g, n))
                            link(dve.scalar_tensor_tensor(rn[:], vh[:, h, :], 2.0, rn[:], ALU.add, ALU.mult))
                            dve.tensor_tensor(vh[:, h, :], acc[:, h % 2, :], rn[:], ALU.mult).then_inc(out_ok, 1)
                        elif kind == "gm":
                            src = full(("gt",))
                            for t in range(TT):
                                ins = dve.tensor_tensor(lg[:, t, :], src[:, t * GC:(t + 1) * GC], bg[:], ALU.add)
                            ins.then_inc(emptied["dve"], 1)
                            wait_emptied(dve, ("gt",))
                            dve.tensor_reduce(gm[:, :, 0], lg[:, :, 0:NE], axis=AX.X, op=ALU.max)
                            link(dve.tensor_reduce(gm[:, :, 1], lg[:, :, SH:SH + 2], axis=AX.X, op=ALU.max))
                            dve.tensor_tensor(lg[:, :, 0:NE], lg[:, :, 0:NE], gm[:, :, 0:1].to_broadcast([P, TT, NE]), ALU.subtract)
                            dve.tensor_tensor(lg[:, :, SH:SH + 2], lg[:, :, SH:SH + 2], gm[:, :, 1:2].to_broadcast([P, TT, 2]), ALU.subtract).then_inc(gates_in, 1)
                            dve.wait_ge(gates_exp, 1)
                            for t in range(TT):
                                dve.max(top[:, t, :], eg[:, t, 0:NE])
                            dve.tensor_reduce(g1[:, 0], eg[:, :, 0:NE], axis=AX.X, op=ALU.add)
                            link(dve.tensor_reduce(g1[:, 1], eg[:, :, SH:SH + 2], axis=AX.X, op=ALU.add))
                            link(dve.tensor_reduce(g1[:, 2], top[:, :, 0:TOPK], axis=AX.X, op=ALU.add))
                            link(dve.reciprocal(g1[:, 0:2], g1[:, 0:2]))
                            dve.tensor_tensor(g1[:, 2], g1[:, 2], g1[:, 0], ALU.mult)
                            dve.tensor_tensor(sw[:, :, 0], eg[:, :, SH], g1[:, 1], ALU.mult)
                            link(dve.tensor_tensor(sw[:, :, 1], eg[:, :, SH + 1], g1[:, 1], ALU.mult))
                            link(dve.tensor_tensor(g1[:, 3], sw[:, :, 0], sw[:, :, 1], ALU.add))
                            dve.scalar_tensor_tensor(g1[:, 0], g1[:, 3], 2.0, sw[:, :, 0], ALU.mult, ALU.mult)
                            link(dve.scalar_tensor_tensor(g1[:, 1], g1[:, 2], 2.0 * TOPK, sw[:, :, 1], ALU.mult, ALU.mult))
                            link(dve.tensor_tensor(g1[:, 0], g1[:, 0], g1[:, 1], ALU.add))
                            link(dve.tensor_scalar(sc[:], g1[:, 0], tg[:, 0:1], None, ALU.mult))
                        elif kind == "op":
                            t = it[1]
                            src = full(it)
                            dve.wait_ge(biased, t + 1)
                            by = sc[:, t:t + 1] if ffn else tg[:, 0:1]
                            x = xs[:, t % (TT // 2), :]
                            dve.scalar_tensor_tensor(x, src, by, x, ALU.mult, ALU.add).then_inc(emptied["dve"], 1)

            for s in made:
                nc.sync.sem_clear(s)
            nc.all_engine_barrier()

        one = lambda a, i: None if a is None else a[i:i + 1]
        turn(schedule(ph, False, True), None, None, one(x_in, 0), one(ctxT, 0))
        x_later, ctx_later = x_in[1:B], None if ctxT is None else ctxT[1:B]
        with nc.Fori(0, B - 1) as b:
            at = bass.ds(b, 1)
            turn(schedule(ph, True, True), x_in[at], x_out[at], x_later[at], None if ctxT is None else ctx_later[at])
        turn(schedule(ph, True, False), x_in[B - 1:B], x_out[B - 1:B], None, None)
        for s in (c_in, c_ms, c_act, c_dve, c_abs):
            nc.sync.sem_clear(s)
        nc.all_engine_barrier()


def build(nc, x, ctxT, weights, g_xattn, g_ffn, xattn_bo, bq, bk, bv, bp, wg, bg, temp, emb, out):
    w_split = nc.dram_tensor("w_split", [8, 2, NG, P, NG, P], F32).ap()
    x1 = nc.dram_tensor("x_after_xattn", [B, N, DM], F32).ap()
    split_weights(nc, weights, w_split)
    attention_phase(nc, Phase(False), x, ctxT, w_split, xattn_bo, g_xattn, x1, {})
    attention_phase(nc, Phase(True), x1, None, w_split, bp, g_ffn, out,
                    dict(bq=bq, bk=bk, bv=bv, wg=wg, bg=bg, temp=temp, emb=emb))


def kernel(**inputs):
    import numpy as np
    import concourse.bacc as bacc
    from concourse.bass_utils import run_bass_kernel_spmd

    a = {k: np.asarray(v) for k, v in inputs.items()}
    pad = lambda w: np.concatenate([w, np.zeros((DM - w.shape[0], DM), w.dtype)]) if w.shape[0] < DM else w
    channels = lambda v: np.ascontiguousarray(v.reshape(NG, P).T)
    zero = np.zeros(1, np.float32)
    arrays = {
        "x": a["x"],
        "ctxT": np.ascontiguousarray(a["ctx_768"].transpose(0, 2, 1)),
        "weights": np.stack([a["L0_xattn_Wq"], pad(a["L0_xattn_Wk"]), pad(a["L0_xattn_Wv"]), a["L0_xattn_Wo"],
                             a["L0_ffn_Wq"].T, a["L0_ffn_Wk"].T, a["L0_ffn_Wv"].T, a["L0_ffn_Wp"].T]),
        "g_xattn": a["g_xattn"], "g_ffn": a["g_ffn"], "xattn_bo": a["L0_xattn_bo"],
        "bq": channels(a["L0_ffn_bq"]), "bk": channels(a["L0_ffn_bk"]), "bv": a["L0_ffn_bv"], "bp": a["L0_ffn_bp"],
        "wg": np.concatenate([a["L0_ffn_Wr"].T, np.zeros((DM, 1), np.float32), a["L0_ffn_Ws"].T], axis=1),
        "bg": np.concatenate([a["L0_ffn_br"], zero, a["L0_ffn_bs"]]),
        "temp": np.ascontiguousarray(a["L0_ffn_temperature"].reshape(NG, NG).T),
        "emb": channels(a["L0_ffn_query_embedding"].reshape(-1)),
    }
    nc = bacc.Bacc("TRN2", target_bir_lowering=False, num_devices=1, dynamic_dma_scratch_size=1024)
    feed, args = {}, []
    for name, arr in arrays.items():
        arr = np.ascontiguousarray(arr)
        feed[f"in_{name}"] = arr
        args.append(nc.dram_tensor(f"in_{name}", arr.shape, mybir.dt.from_np(arr.dtype), kind="ExternalInput").ap())
    out = nc.dram_tensor("out", [B, N, DM], F32, kind="ExternalOutput").ap()
    build(nc, *args, out)
    return run_bass_kernel_spmd(nc, [feed], core_ids=[0]).results[0]["out"]
```

```python
from contextlib import ExitStack

import concourse.bass as bass
from concourse import mybir

F32 = mybir.dt.float32
F32R = mybir.dt.float32r
ACT = mybir.ActivationFunctionType
ALU = mybir.AluOpType
AX = mybir.AxisListType

B, N, DM, DC = 8, 1024, 512, 384
P = 128
TT = N // P
HALF = N // 2
NG = DM // P
STEPS = 2 * TT
EPS = 1e-5
NE = 15
GC = 18
SH = 16
TOPK = 3


class Phase:

    def __init__(self, ffn):
        self.ffn = ffn
        self.D = 32 if ffn else 64
        self.G = P // self.D
        self.PAIRS = self.G // 2
        self.KC = (DM if ffn else DC) // P
        self.W = 4 if ffn else 0
        self.SCALE = float(self.D) ** -0.5
        self.SLOTS = 2 if ffn else 4
        self.MROW = 96 if ffn else 64
        self.NP = 10 if ffn else 8
        self.ADDER = ["dve", "pool", "pool", "pool"] if ffn else ["pool", "dve"]
        self.MX0 = 2
        self.SUM = 32 if ffn else 64

    def q_copies(self):
        return [("hi", 0, 0), ("lo", 32, 0), ("hi", 64, 0)] if self.ffn else [("hi", 0, 0), ("lo", 64, 0), ("hi", 0, 1)]

    def k_copies(self):
        return [("hi", 0, 1), ("hi", 32, 1), ("lo", 64, 1)] if self.ffn else [("hi", 0, 2), ("hi", 64, 2), ("lo", 0, 3)]

    def max_operands(self):
        return (0, 1, 96) if self.ffn else (0, 2, 128)

    def score_passes(self):
        return [(1, 0)] if self.ffn else [(2, 0), (3, 1)]

    def m_stack(self):
        return 0 if self.ffn else 1

    def one_stack(self):
        return 1 if self.ffn else 3



def maxima(ph, g):
    return [("mx", g, e, t, j) for e in range(ph.G) for t in range(TT) for j in range(2)]


def chunks(ph, kind):
    return ph.KC if kind == "pk" else NG


def projected(ph, g, kind):
    s = []
    for n in range(2):
        s += [(kind, g, n, c) for c in range(chunks(ph, kind))]
        if kind == "pq" and ph.ffn:
            s += [None, None, ("ss", g, n), None, None, None, ("s2", g, n), None, None, ("s3", g, n)]
        else:
            s += [None, (kind + "l", g, n), None]
    return s


def normalised(ph):
    gap = lambda n: [None] * n
    s = [("xl", 2)] if ph.ffn else [("xl", 0)] + gap(4) + [("cx", 0)] + gap(3) + [("xl", 1)] + gap(5) + [("cx", 1)] + gap(2) + [("xl", 2)]
    s += gap(5)
    for n in range(2):
        s += [("ln", n), None, None, ("l2", n), None, None]
        for k in range(NG):
            s += [("tr", n, k), None, ("trl", n, k), None]
        if n == 0:
            s += [("xl", 3)] + gap(5)
    return s


def spread(slots, items, first, last):
    for i, it in enumerate(items):
        if it:
            slots[first + i * (last - first) // len(items)].append(it)


def schedule(ph, this, following):
    if not this:
        s = [it for it in [("wl", 0)] + normalised(ph) + projected(ph, 0, "pq") + projected(ph, 0, "pk") if it]
        return s + [("sd", 0), ("wl", 1)] + maxima(ph, 0) + [("nm", 0), ("mt", 0), ("ml", 0), ("md", 0)]
    s = [("wv", 0)]
    per = ph.G + 1
    tail, held = [], None
    s += [("S", 0, e) for e in range(ph.G)]
    s += [it for it in projected(ph, 1, "pq") + projected(ph, 1, "pk") if it] + [("sd", 1), ("wl", 2), ("vp", 0)]
    for g in range(NG):
        slots = [[] for _ in range(per * STEPS)]
        if g == 0:
            for t in range(1, TT):
                slots[(t - 1) * per + 1] += [("vp", t)]
            slots[(TT - 1) * per] += [("wo", 0)]
        if g + 1 < NG:
            spread(slots, maxima(ph, g + 1), ph.MX0 * per, (STEPS - 2) * per)
            slots[(STEPS - 2) * per] += [("nm", g + 1)]
            slots[(STEPS - 2) * per + 1] += [("mt", g + 1), ("ml", g + 1), ("md", g + 1)]
        if g + 2 < NG:
            spread(slots, projected(ph, g + 2, "pq") + projected(ph, g + 2, "pk"), 3 * per, STEPS * per - 2)
            slots[-1] += [("wl", (g + 3) % NG)] if g + 3 < NG or following else []
            if g == 1 and following:
                slots[8 * per] += normalised(ph)[:1]
        elif g == 2 and following:
            spread(slots, normalised(ph)[1:], 0, STEPS * per - per)
        elif g == 3 and following:
            spread(slots, projected(ph, 0, "pq") + projected(ph, 0, "pk"), 0, 4 * per)
            slots[4 * per] += [("sd", 0), ("wl", 1)]
            m = maxima(ph, 0)
            now = len(m) * 7 // 8
            spread(slots, m[:now], 6 * per, STEPS * per)
            tail = m[now:] + [("nm", 0), ("mt", 0), ("ml", 0), ("md", 0)]
        for st in range(STEPS):
            T = g * STEPS + st
            for e in range(ph.G):
                if T + 1 < NG * STEPS:
                    s += [("S", T + 1, e)]
                here = slots[st * per + e]
                if held is not None and e < 1:
                    held += here
                elif held is not None:
                    s += [("ev", held_half // 2, held_half % 2)] + held + here
                    held = None
                else:
                    s += here
            s += [("ad", T), ("PV", T)]
            here = slots[st * per + ph.G]
            h = T // TT - 1
            if T % TT == 0 and h >= 0:
                s += [("sm", h // 2, h % 2)] + here[:1]
                held, held_half = here[1:], h
            else:
                s += here
        if g + 2 < NG:
            s += [("sd", g + 2)]
    first, second = range(TT // 2), range(TT // 2, TT)
    last_sum = [("sm", NG - 1, 1), ("ev", NG - 1, 1)]
    share = -(-len(tail) // (TT + 2))
    some = lambda: [tail.pop(0) for _ in range(min(share, len(tail)))]
    s += [("xr", 0)]
    if ph.ffn:
        for part in (first, second):
            for t in part:
                s += ([("hs", t)] if part == first else []) + some() + [("gt", t)]
            if part == first:
                s += some() + last_sum + some()
        s += tail + [("gm", 0)]
        for t in range(TT):
            s += [("xb", t), ("op", t)] + ([("hs", t + 4)] if t + 4 < TT else [])
    else:
        for part in (first, second):
            for t in part:
                s += [("hs", t)] + some() + [("xb", t), ("op", t)]
            if part == first:
                s += some() + last_sum + some()
        s += tail
    return s


class Order:

    def __init__(self, ph, items):
        self.items = items
        self.pos = {it: i for i, it in enumerate(items)}
        assert len(self.pos) == len(items)
        lower = {"tr": "trl", "pk": "pkl", "ss": "s2", "mt": "ml", "sm": "ev"}
        if not ph.ffn:
            lower["pq"] = "pql"
        by_act = ("pq",) if ph.ffn else ("vp",)
        self.bank, self.before, self.full, self.first, emptied = {}, {}, {}, {}, {}
        last, used = [None] * 3, [-3, -2, -1]
        for at, it in enumerate(items):
            kind = it[0]
            if kind not in ("tr", "pq", "pk", "ss", "vp", "mx", "mt", "sm", "gt", "op"):
                continue
            unit = self.unit(it)
            if unit not in self.bank:
                ring = {"mx": (0, 1), "sm": (0, 1), "mt": (0, 1), "vp": (0, 1), "op": (0, 1, 2)}.get(kind, (2,))
                b = min(ring, key=lambda x: used[x])
                self.bank[unit], self.before[unit], self.first[unit] = b, last[b], at
                last[b] = unit
            used[self.bank[unit]] = at
            if (kind in ("pq", "pk") and it[3] < chunks(ph, kind) - 1) or (kind == "gt" and it[1] < TT - 1):
                continue
            self.full[unit] = len(self.full) + 1
            emptied[("gm", 0) if kind == "gt" else (lower[kind],) + unit[1:] if kind in lower else it] = unit
        counts = {"act": 0, "dve": 0}
        self.drained = {}
        where = {}
        for at, it in enumerate(items):
            if it in emptied:
                engine = "act" if it[0] in by_act else "dve"
                counts[engine] += 1
                self.drained[emptied[it]] = (engine, counts[engine])
                where[emptied[it]] = at
        for unit, prior in self.before.items():
            assert prior is None or where[prior] < self.first[unit]

    @staticmethod
    def unit(it):
        return ("gt",) if it[0] == "gt" else it[:3] if it[0] in ("pq", "pk") else it

    def nth(self, it, by, same=lambda x: True):
        if it not in self.pos or self.pos[it] > self.pos[by]:
            return 0
        return [x for x in self.items if x[0] == it[0] and same(x)].index(it) + 1

    def so_far(self, kind, by, same=lambda x: True):
        return sum(1 for x in self.items[:self.pos[by]] if x[0] == kind and same(x))


def split_weights(nc, weights, w_split):
    GROUP = 4
    with ExitStack() as ctx:
        sb = lambda name, shape, dt: ctx.enter_context(nc.sbuf_tensor(name, shape, dt))
        sem = lambda name: ctx.enter_context(nc.semaphore(name))
        raw = sb("w_raw", [P, GROUP, NG, DM], F32)
        hi = sb("w_hi", [P, GROUP, NG, DM], F32R)
        lo = sb("w_lo", [P, GROUP, NG, DM], F32R)
        raw_in = [sem(f"w_raw_in{i}") for i in range(GROUP)]
        hi_ok, lo_ok, out_ok = sem("w_hi_ok"), sem("w_lo_ok"), sem("w_out_ok")
        source = weights.rearrange("(a i) (k p) c -> p a i k c", i=GROUP, p=P)
        target = w_split.rearrange("(a i) h g p k c -> p a i h g (k c)", i=GROUP)
        with nc.Fori(0, 8 // GROUP) as turn:
            at = bass.ds(turn, 1)
            with nc.Block() as block:

                @block.sync
                def _(sp):
                    for i in range(GROUP):
                        sp.dma_start(raw[:, i], source[:, at, i].rearrange("p a k c -> p (a k) c")).then_inc(raw_in[i], 16)
                    for i in range(GROUP):
                        for part, (src, ok) in enumerate(((hi, hi_ok), (lo, lo_ok))):
                            sp.wait_ge(ok, i + 1)
                            for g in range(NG):
                                sp.dma_start(target[:, at, i, part, g].rearrange("p a (k c) -> p (a k) c", k=NG),
                                             src[:, i, :, g * P:(g + 1) * P].bitcast(F32)).then_inc(out_ok, 16)
                    sp.wait_ge(out_ok, GROUP * 2 * NG * 16)

                @block.scalar
                def _(act):
                    for i in range(GROUP):
                        act.wait_ge(raw_in[i], 16)
                        act.activation(hi[:, i], raw[:, i], ACT.Copy).then_inc(hi_ok, 1)

                @block.vector
                def _(dve):
                    for i in range(GROUP):
                        dve.wait_ge(raw_in[i], 16)
                        dve.wait_ge(hi_ok, i + 1)
                        dve.tensor_tensor(lo[:, i], raw[:, i], hi[:, i].bitcast(F32), ALU.subtract).then_inc(lo_ok, 1)

            for s in raw_in + [hi_ok, lo_ok, out_ok]:
                nc.sync.sem_clear(s)
            nc.all_engine_barrier()


def attention_phase(nc, ph, x_in, ctxT, w_split, bias_row, gate_scalar, x_out, small):
    ffn, D, G, KC = ph.ffn, ph.D, ph.G, ph.KC
    NCOPY = 6 * 16
    HALVES = 2 * NG
    LAST_ADDED = NG * STEPS - 3
    pre = "f_" if ffn else "x_"
    with ExitStack() as ctx:
        sb = lambda name, shape, dt=F32: ctx.enter_context(nc.sbuf_tensor(pre + name, shape, dt))
        made = []

        def sem(name, cleared=True):
            s = ctx.enter_context(nc.semaphore(pre + name))
            if cleared:
                made.append(s)
            return s

        xs = sb("xs", [P, TT // 2, DM])
        raw = xs[:].rearrange("p (t a) d -> p t (a d)", a=2)
        xT_hi = sb("xT_hi", [P, NG, N], F32R)
        xT_lo = sb("xT_lo", [P, NG, N], F32R)
        if ffn:
            kv_hi, kv_lo = xT_hi, xT_lo
        else:
            kv_hi = sb("kv_hi", [P, KC, N], F32R)
            kv_lo = sb("kv_lo", [P, KC, N], F32R)
        wqk = sb("wqk", [P, 2, 2, NG, P], F32R)
        wvo = sb("wvo", [P, 2, NG, NG, P], F32R)
        stack = sb("stack", [P, 2, G * ph.SLOTS, N], F32R)
        cq = {h: sb(f"cq_{h}", [P, N], F32R) for h in ("hi", "lo")}
        ck = {h: sb(f"ck_{h}", [P, N], F32R) for h in ("hi", "lo")}
        vh = sb("vh", [P, HALVES + 1, HALF])
        v = vh[:, 1:HALVES + 1, :].rearrange("p (g a) c -> p g (a c)", a=2)
        probs = sb("probs", [P, ph.NP, HALF])
        NACC = 2 * G
        added = sb("added", [P, NACC, HALF])
        rn = sb("rn", [P, HALF])
        mx = sb("mx", [P, G * TT, 2])
        nm = sb("nm", [P, G * TT])
        mrow = sb("mrow", [G * TT, P], F32R)
        ident = sb("ident", [P, P])
        ones = sb("ones", [P, ph.SUM])
        bo = sb("bo", [P, DM])
        tg = sb("tg", [P, 1])
        st = sb("st", [P, TT, 6])
        mv = sb("mv", [P, TT, 2])
        rs = sb("rs", [P, 3, TT])
        if ffn:
            qb = sb("qb", [P, 2, HALF])
            sq = sb("sq", [P, 2, HALF])
            qy = sb("qy", [P, 2, HALF])
            blk = sb("blk", [P, P])
            bq, bk = sb("bq", [P, NG]), sb("bk", [P, NG])
            emb, tau, et = sb("emb", [P, NG]), sb("tau", [P, NG]), sb("et", [P, NG])
            tmp = sb("tmp", [P, 3, NG])
            bv = sb("bv", [P, DM])
            wg = sb("wg", [P, NG, GC])
            bg = sb("bg", [P, GC])
            lg = sb("lg", [P, TT, GC])
            eg = sb("eg", [P, TT, GC])
            gm = sb("gm", [P, TT, 2])
            top = sb("top", [P, TT, 8])
            g1 = sb("g1", [P, 4, TT])
            sw = sb("sw", [P, TT, 2])
            sc = sb("sc", [P, TT])
        acc = ctx.enter_context(nc.psum_tensor(pre + "acc", [P, 2, HALF], F32))
        scores = ctx.enter_context(nc.psum_tensor(pre + "scores", [P, 3, HALF], F32))
        aux = ctx.enter_context(nc.psum_tensor(pre + "aux", [P, 3, HALF], F32))

        def split_slot(t):
            c = cq if t % 4 < 2 else ck
            return [c[half][:, t % 2 * HALF:(t % 2 + 1) * HALF].rearrange("p (g c) -> p g c", g=NG) for half in ("hi", "lo")]

        def outputs(t):
            first = t // (TT // 2)
            pieces = vh[:, 0:HALVES, :].rearrange("p (g n) c -> p g n c", n=2)
            return pieces[:, :, first, t % (TT // 2) * P:(t % (TT // 2) + 1) * P]

        def exp_buffer(T, e):
            if T % TT == 0:
                return added[:, (T // TT % 2) * G + e, :], None
            m = (T - T // TT - 1) * G + e
            prior = None
            if m >= ph.NP:
                s, head = divmod(m - ph.NP, G)
                prior = (s + s // (TT - 1) + 1, head)
            return probs[:, m % ph.NP, :], prior

        def adds(T, e):
            mine = [h for h in range(G) if ph.ADDER[h] == ph.ADDER[e]]
            return (T - T // TT - 1) * len(mine) + mine.index(e) + 1

        c_in, c_ms, c_act, c_dve = (sem(n, False) for n in ("c_in", "c_ms", "c_act", "c_dve"))
        c_abs, c_pool = sem("c_abs", False), sem("c_pool", False)
        n_const = 2 + (2 + 3 + 1 + G if ffn else 0)

        def clear_stacks(eng, link, par):
            for e in range(G):
                for slot in (ph.m_stack(), ph.one_stack()):
                    link(eng.memset(stack[ph.MROW:P, par, e * ph.SLOTS + slot, :].bitcast(F32), 0.0))
                link(eng.memset(stack[ph.MROW:ph.MROW + 1, par, e * ph.SLOTS + ph.one_stack(), :].bitcast(F32), 1.0))

        with nc.Block() as block:

            @block.sync
            def _(sp):
                sp.dma_start(tg[:], gate_scalar.partition_broadcast(P)).then_inc(c_in, 16)
                sp.dma_start(bo[:], bias_row.partition_broadcast(P)).then_inc(c_in, 16)
                if ffn:
                    sp.dma_start(bv[:], small["bv"].partition_broadcast(P)).then_inc(c_in, 16)
                    sp.dma_start(bg[:], small["bg"].partition_broadcast(P)).then_inc(c_in, 16)
                    for dst, name in ((bq, "bq"), (bk, "bk"), (emb, "emb")):
                        sp.dma_start(dst[:], small[name]).then_inc(c_in, 16)
                    sp.dma_start(wg[:], small["wg"].rearrange("(k p) c -> p k c", p=P)).then_inc(c_in, 16)
                    for e in range(G):
                        sp.dma_start(tau[e * D:(e + 1) * D, :], small["temp"][e].partition_broadcast(D)).then_inc(c_in, 16)

            @block.gpsimd
            def _(pool):
                pool.memset(ident[:], 0.0).then_inc(c_ms, 1)
                pool.memset(ones[:], 1.0).then_inc(c_ms, 1)
                pool.wait_ge(c_ms, 2)
                pool.affine_select(out=ident[:], in_=ident[:], compare_op=ALU.not_equal, fill=1.0, base=0,
                                   pattern=[[-1, P]], channel_multiplier=1).then_inc(c_ms, 1)
                pool.wait_ge(c_ms, 3)
                done = [0]

                def link(ins):
                    done[0] += 1
                    ins.then_inc(c_pool, 1)
                    pool.wait_ge(c_pool, done[0])

                clear_stacks(pool, link, 1)

            @block.vector
            def _(dve):
                done = [0]

                def link(ins):
                    done[0] += 1
                    ins.then_inc(c_dve, 1)
                    dve.wait_ge(c_dve, done[0])

                clear_stacks(dve, link, 0)
                if ffn:
                    link(dve.memset(blk[:], 0.0))
                    for e in range(G):
                        link(dve.memset(blk[e * D:(e + 1) * D, e * D:(e + 1) * D], 1.0))
                dve.wait_ge(c_act, 1)
                link(dve.tensor_scalar(bo[:], bo[:], tg[:, 0:1], None, ALU.mult))
                if ffn:
                    link(dve.tensor_scalar(tmp[:, 0], tau[:], -1.0, None, ALU.mult))
                    dve.tensor_tensor(tmp[:, 0], tau[:], tmp[:, 0], ALU.min).then_inc(c_abs, 1)
                    dve.wait_ge(c_act, 3)
                    link(dve.tensor_scalar(tau[:], tau[:], 0.0, None, ALU.max))
                    link(dve.tensor_tensor(tau[:], tau[:], tmp[:, 2], ALU.add))
                    link(dve.tensor_tensor(et[:], emb[:], tau[:], ALU.mult))

            @block.scalar
            def _(act):
                act.wait_ge(c_in, 16 * n_const)
                act.activation(tg[:], tg[:], ACT.Tanh).then_inc(c_act, 1)
                act.preload_act_table_set("natural_log_exp_and_others")
                if ffn:
                    act.wait_ge(c_abs, 1)
                    act.activation(tmp[:, 1], tmp[:, 0], ACT.Exp).then_inc(c_act, 1)
                    act.wait_ge(c_act, 2)
                    act.activation(tmp[:, 2], tmp[:, 1], ACT.Ln, bias=1.0).then_inc(c_act, 1)

        xs_loaded = [sem(f"xs_loaded{i}") for i in range(4)]
        x_again = [sem(f"x_again{i}") for i in range(TT)]
        stored = [sem(f"stored{i}") for i in range(TT)]
        w_loaded, wv_loaded, wo_loaded = sem("w_loaded"), sem("wv_loaded"), sem("wo_loaded")
        stacked = [[sem(f"stacked{i}_{e}") for e in range(G)] for i in range(2)]
        m_stacked = [sem(f"m_stacked{i}") for i in range(2)]
        ctx_hi_ok, ctx_lo_ok = sem("ctx_hi_ok"), sem("ctx_lo_ok")
        normed = sem("normed")
        norm_in = sem("norm_in")
        rstd_in, rstd_ok = sem("rstd_in"), sem("rstd_ok")
        aux_full = sem("aux_full")
        emptied = {"act": sem("emptied_by_act"), "dve": sem("emptied_by_dve")}
        hi_ok = sem("hi_ok")
        sq_ok, y_ok, qn_ok, qs_ok, qlo_ok = (sem(n) for n in ("sq_ok", "y_ok", "qn_ok", "qs_ok", "qlo_ok"))
        nm_ok = sem("nm_ok")
        scored, probs_ok, weighed = sem("scored"), sem("probs_ok"), sem("weighed")
        added_ok = {"dve": sem("added_by_dve"), "pool": sem("added_by_pool")}
        rinv_ok, out_ok = sem("rinv_ok"), sem("out_ok")
        h_hi_ok, h_lo_ok, biased = sem("h_hi_ok"), sem("h_lo_ok"), sem("biased")
        gates_in, gates_exp = sem("gates_in"), sem("gates_exp")
        act_chain, dve_chain = sem("act_chain"), sem("dve_chain")

        def turn(sched, x_this, out_this, x_next, ctx_next):
            o = Order(ph, sched)
            MAKES_HI = ("tr", "pk") if ffn else ("tr", "pk", "pq")
            hi_units = [u for u in o.full if u[0] in MAKES_HI]
            q_units = [u for u in o.full if u[0] == "pq"]
            ends = lambda it: it[0] not in ("pq", "pk") or it[3] == chunks(ph, it[0]) - 1
            mine = lambda g: lambda x: x[1] % 2 == g % 2

            def wait_full(eng, unit):
                eng.wait_ge(aux_full, o.full[unit])

            def wait_emptied(eng, unit):
                who, n = o.drained[unit]
                eng.wait_ge(emptied[who], n)

            def wait_stacked(eng, g, e, by):
                n = o.nth(("sd", g), by, mine(g))
                if n:
                    eng.wait_ge(stacked[g % 2][e], NCOPY * n)

            def wait_copies_left(eng, by):
                before = [x for x in sched[:o.pos[by]] if x[0] == "sd"]
                if before:
                    for e in range(G):
                        wait_stacked(eng, before[-1][1], e, by)

            with nc.Block() as block:

                @block.sync
                def _(sp):
                    for it in sched:
                        kind, g = it[0], it[1]
                        if kind == "xl":
                            if g < 2:
                                if g:
                                    sp.wait_ge(ctx_lo_ok, 1)
                                tiles = slice(2 * g, min(2 * g + 2, KC))
                                sp.dma_start(raw[:, 0:tiles.stop - tiles.start, :],
                                             ctx_next.rearrange("a (k p) n -> p (a k) n", p=P)[:, tiles, :]).then_inc(xs_loaded[g], 16)
                            else:
                                if g == 3:
                                    wait_full(sp, ("tr", 0, NG - 1))
                                elif not ffn:
                                    sp.wait_ge(ctx_lo_ok, KC)
                                sp.dma_start(xs[:], x_next.rearrange("a (t p) d -> p (a t) d", p=P)[:, (g - 2) * TT // 2:(g - 1) * TT // 2, :]).then_inc(xs_loaded[g], 16)
                        elif kind == "wl":
                            before = [x for x in sched[:o.pos[it]] if x[0] == "pk"]
                            if before:
                                wait_full(sp, before[-1][:3])
                            for what in range(2):
                                for part in range(2):
                                    sp.dma_start(wqk[:, what, part].bitcast(F32), w_split[ph.W + what, part, g]).then_inc(w_loaded, 16)
                        elif kind in ("wv", "wo"):
                            if kind == "wo":
                                wait_full(sp, ("vp", TT - 1))
                            w, done = (ph.W + 2, wv_loaded) if kind == "wv" else (ph.W + 3, wo_loaded)
                            for part in range(2):
                                sp.dma_start(wvo[:, part].bitcast(F32), w_split[w, part].rearrange("g p k c -> p k g c")).then_inc(done, 16)
                        elif kind == "sd":
                            steps = [x[1] for x in sched[:o.pos[it]] if x[0] == "S" and x[1] // STEPS % 2 == g % 2]
                            if steps:
                                sp.wait_ge(scored, (max(steps) + 1) * G)
                            if ffn:
                                sp.wait_ge(qlo_ok, q_units.index(("pq", g, 1)) + 1)
                            else:
                                wait_emptied(sp, ("pq", g, 1))
                            wait_emptied(sp, ("pk", g, 1))
                            for e in range(G):
                                for src, copies in ((cq, ph.q_copies()), (ck, ph.k_copies())):
                                    for half, row, slot in copies:
                                        sp.dma_start(stack[row:row + D, g % 2, e * ph.SLOTS + slot, :].bitcast(F32),
                                                     src[half][e * D:(e + 1) * D, :].bitcast(F32)).then_inc(stacked[g % 2][e], 16)
                        elif kind == "md":
                            wait_emptied(sp, ("mt", g))
                            for e in range(G):
                                dst = stack[ph.MROW:ph.MROW + 1, g % 2, e * ph.SLOTS + ph.m_stack(), :]
                                sp.dma_start(dst.rearrange("o (t q) -> o t q", q=P).bitcast(F32),
                                             mrow[e * TT:(e + 1) * TT, :].bitcast(F32)).then_inc(m_stacked[g % 2], 16)
                        elif kind == "xr":
                            if ("tr", 1, NG - 1) in o.full:
                                wait_full(sp, ("tr", 1, NG - 1))
                            for t in range(TT // 2):
                                sp.dma_start(xs[:, t, :], x_this.rearrange("a (t p) d -> p (a t) d", p=P)[:, t, :]).then_inc(x_again[t], 16)
                        elif kind == "op":
                            t = g
                            wait_emptied(sp, it)
                            sp.dma_start(out_this.rearrange("a (t p) d -> p (a t) d", p=P)[:, t, :], xs[:, t % (TT // 2), :]).then_inc(stored[t], 16)
                            if t < TT // 2:
                                sp.wait_ge(stored[t], 16)
                                sp.dma_start(xs[:, t, :], x_this.rearrange("a (t p) d -> p (a t) d", p=P)[:, t + TT // 2, :]).then_inc(x_again[t + TT // 2], 16)
                    sp.wait_ge(w_loaded, 64 * sum(x[0] == "wl" for x in sched))
                    for i in range(2):
                        rows = sum(x[0] == "md" and x[1] % 2 == i for x in sched)
                        if rows:
                            sp.wait_ge(m_stacked[i], G * 16 * rows)
                    if x_this is not None:
                        for t in range(TT // 2, TT):
                            sp.wait_ge(stored[t], 16)

                def add(eng, name, T):
                    for e in range(G):
                        if ph.ADDER[e] != name:
                            continue
                        onto, _ = exp_buffer(T - T % TT, e)
                        eng.wait_ge(probs_ok, T * G + e + 1)
                        if T % TT == 1:
                            eng.wait_ge(weighed, T)
                        else:
                            eng.wait_ge(added_ok[name], adds(T - 1, e))
                        eng.tensor_tensor(onto, onto, exp_buffer(T, e)[0], ALU.add).then_inc(added_ok[name], 1)

                @block.gpsimd
                def _(pool):
                    for it in sched:
                        kind = it[0]
                        if kind == "cx":
                            for k in range(2 * it[1], min(2 * it[1] + 2, KC)):
                                pool.wait_ge(ctx_hi_ok, k + 1)
                                pool.tensor_tensor(kv_lo[:, k, :], raw[:, k % 2, :], kv_hi[:, k, :].bitcast(F32), ALU.subtract).then_inc(ctx_lo_ok, 1)
                        elif kind == "s3":
                            _, g, n = it
                            pool.wait_ge(qs_ok, 2 * q_units.index(("pq", g, n)) + 2)
                            q = slice(n * HALF, (n + 1) * HALF)
                            pool.tensor_tensor(cq["lo"][:, q], qy[:, n], cq["hi"][:, q].bitcast(F32), ALU.subtract).then_inc(qlo_ok, 1)
                        elif kind == "ad" and it[1] % TT and it[1] <= LAST_ADDED:
                            add(pool, "pool", it[1])
                        elif kind == "xb":
                            t = it[1]
                            pool.wait_ge(x_again[t], 16)
                            pool.tensor_tensor(xs[:, t % (TT // 2), :], xs[:, t % (TT // 2), :], bo[:], ALU.add).then_inc(biased, 1)

                @block.tensor
                def _(pe):
                    def bank(it):
                        unit = o.unit(it)
                        if o.before[unit] and o.first[unit] == o.pos[it]:
                            wait_emptied(pe, o.before[unit])
                        return aux[:, o.bank[unit], :]

                    def product(out, lhs, rhs, tiles, whole):
                        for k in tiles:
                            for i, (a, c) in enumerate(((0, 0), (0, 1), (1, 0))):
                                ins = pe.matmul(out, lhs(a, k), rhs(c, k), start=k == 0 and i == 0, stop=k == whole - 1 and i == 2)
                        return ins

                    xT, kvT = (xT_hi, xT_lo), (kv_hi, kv_lo)

                    def wait_source(keys):
                        if keys and not ffn:
                            if made_context:
                                pe.wait_ge(ctx_lo_ok, KC)
                        elif made_x:
                            wait_emptied(pe, ("tr", 1, NG - 1))

                    made_context = made_x = False
                    for it in sched:
                        kind = it[0]
                        if kind == "cx":
                            made_context = it[1] == 1
                        elif kind == "tr":
                            _, n, k = it
                            made_x = (n, k) == (1, NG - 1)
                            pe.wait_ge(normed, n + 1)
                            out = bank(it)
                            for i in range(TT // 2):
                                ins = pe.transpose(out[:, i * P:(i + 1) * P], xs[:, i, k * P:(k + 1) * P], ident[:])
                            ins.then_inc(aux_full, 1)
                        elif kind in ("pq", "pk"):
                            _, g, n, c0 = it
                            what = int(kind == "pk")
                            if c0 == 0:
                                loads = o.nth(("wl", g), it)
                                if loads:
                                    pe.wait_ge(w_loaded, 64 * loads)
                                wait_source(what)
                            src = kvT if what else xT
                            q = slice(n * HALF, (n + 1) * HALF)
                            ins = product(bank(it), lambda a, k: wqk[:, what, a, k, :], lambda c, k: src[c][:, k, q], [c0], chunks(ph, kind))
                            if ends(it):
                                ins.then_inc(aux_full, 1)
                        elif kind == "ss":
                            _, g, n = it
                            out = bank(it)
                            pe.wait_ge(sq_ok, q_units.index(("pq", g, n)) + 1)
                            pe.matmul(out, blk[:], sq[:, n], start=True, stop=True).then_inc(aux_full, 1)
                        elif kind == "vp":
                            t = it[1]
                            pe.wait_ge(wv_loaded, 32)
                            r = slice(t * P, (t + 1) * P)
                            product(bank(it), lambda a, k: kvT[a][:, k, r], lambda c, k: wvo[:, c, k].rearrange("p g c -> p (g c)"),
                                    range(KC), KC).then_inc(aux_full, 1)
                        elif kind == "mx":
                            _, g, e, t, j = it
                            qs, ks, rows = ph.max_operands()
                            out = bank(it)
                            wait_stacked(pe, g, e, it)
                            pe.matmul(out, stack[0:rows, g % 2, e * ph.SLOTS + qs, t * P:(t + 1) * P],
                                      stack[0:rows, g % 2, e * ph.SLOTS + ks, j * HALF:(j + 1) * HALF],
                                      start=True, stop=True).then_inc(aux_full, 1)
                        elif kind == "mt":
                            g = it[1]
                            out = bank(it)
                            pe.wait_ge(nm_ok, o.nth(("nm", g), it))
                            pe.transpose(out[0:G * TT, 0:P], nm[:], ident[:]).then_inc(aux_full, 1)
                        elif kind == "S":
                            _, T, e = it
                            g, s = divmod(T, STEPS)
                            n, jt = divmod(s, TT)
                            if s == 0 and e == 0 and o.nth(("md", g), it, mine(g)):
                                pe.wait_ge(m_stacked[g % 2], G * 16 * o.nth(("md", g), it, mine(g)))
                            u = T * G + e
                            if u >= 3:
                                pe.wait_ge(probs_ok, u - 2)
                            passes = ph.score_passes()
                            for a, (ks, qs) in enumerate(passes):
                                ins = pe.matmul(scores[:, u % 3, :], stack[:, g % 2, e * ph.SLOTS + ks, jt * P:(jt + 1) * P],
                                                stack[:, g % 2, e * ph.SLOTS + qs, n * HALF:(n + 1) * HALF],
                                                start=a == 0, stop=a == len(passes) - 1)
                            ins.then_inc(scored, 1)
                        elif kind == "PV":
                            T = it[1]
                            h, jt = divmod(T, TT)
                            g = h // 2
                            pe.wait_ge(probs_ok, (T + 1) * G)
                            if T < TT:
                                wait_emptied(pe, ("vp", T))
                            if jt == 0 and h >= 2:
                                pe.wait_ge(out_ok, h - 1)
                            for e in range(G):
                                ins = pe.matmul(acc[e * D:(e + 1) * D, h % 2, :], v[:, g, jt * P + e * D:jt * P + (e + 1) * D],
                                                exp_buffer(T, e)[0], start=jt == 0, stop=jt == TT - 1)
                            ins.then_inc(weighed, 1)
                        elif kind == "sm":
                            _, g, n = it
                            h = 2 * g + n
                            out = bank(it)
                            end = (h + 1) * TT
                            apart = range(min(end, LAST_ADDED + 1), end)
                            for name in ("dve", "pool"):
                                top_head = max(e for e in range(G) if ph.ADDER[e] == name)
                                pe.wait_ge(added_ok[name], adds(min(end - 1, LAST_ADDED), top_head))
                            for e in range(G):
                                terms = [added[:, h % 2 * G + e, :]] + [exp_buffer(T, e)[0] for T in apart]
                                for i, term in enumerate(terms):
                                    ins = pe.matmul(out[e * D:(e + 1) * D, :], ones[:], term, start=i == 0, stop=i == len(terms) - 1)
                            ins.then_inc(aux_full, 1)
                        elif kind == "gt":
                            t = it[1]
                            out = bank(it)
                            pe.wait_ge(out_ok, HALVES - 1 if t < TT // 2 else HALVES)
                            for k in range(NG):
                                ins = pe.matmul(out[:, t * GC:(t + 1) * GC], outputs(t)[:, k, :], wg[:, k, :], start=k == 0, stop=k == NG - 1)
                            if t == TT - 1:
                                ins.then_inc(aux_full, 1)
                        elif kind == "op":
                            t = it[1]
                            out = bank(it)
                            hi_lo = split_slot(t)
                            pe.wait_ge(wo_loaded, 32)
                            pe.wait_ge(h_lo_ok, t + 1)
                            product(out, lambda a, k: hi_lo[a][:, k, :], lambda c, k: wvo[:, c, k].rearrange("p g c -> p (g c)"),
                                    range(NG), NG).then_inc(aux_full, 1)

                @block.scalar
                def _(act):
                    chain = [0]

                    def link(ins):
                        chain[0] += 1
                        ins.then_inc(act_chain, 1)
                        act.wait_ge(act_chain, chain[0])

                    def full(unit):
                        wait_full(act, unit)
                        return aux[:, o.bank[unit], :]

                    for it in sched:
                        kind = it[0]
                        if kind == "cx":
                            act.wait_ge(xs_loaded[it[1]], 16)
                            if it[1] == 0 and ("pk", NG - 1, 1) in o.full:
                                wait_full(act, ("pk", NG - 1, 1))
                            for k in range(2 * it[1], min(2 * it[1] + 2, KC)):
                                act.activation(kv_hi[:, k, :], raw[:, k % 2, :], ACT.Copy).then_inc(ctx_hi_ok, 1)
                        elif kind == "ln":
                            n = it[1]
                            r = slice(n * TT // 2, (n + 1) * TT // 2)
                            act.wait_ge(rstd_in, n + 1)
                            link(act.activation(rs[:, 1, r], rs[:, 0, r], ACT.Ln))
                            act.activation(rs[:, 1, r], rs[:, 1, r], ACT.Exp, scale=-0.5).then_inc(rstd_ok, 1)
                        elif kind == "l2":
                            n = it[1]
                            act.wait_ge(norm_in, n + 1)
                            for t in range(TT // 2):
                                i = n * TT // 2 + t
                                ins = act.activation(xs[:, t, :], xs[:, t, :], ACT.Identity, scale=rs[:, 1, i:i + 1], bias=rs[:, 0, i:i + 1])
                            ins.then_inc(normed, 1)
                        elif kind == "tr":
                            _, n, k = it
                            act.activation(xT_hi[:, k, n * HALF:(n + 1) * HALF], full(it), ACT.Copy).then_inc(hi_ok, 1)
                        elif kind in MAKES_HI and ends(it):
                            _, g, n, _ = it
                            if n == 0:
                                wait_copies_left(act, it)
                            src = full(it[:3])
                            dst = (cq if kind == "pq" else ck)["hi"][:, n * HALF:(n + 1) * HALF]
                            if ffn:
                                act.activation(dst, src, ACT.Identity, bias=bk[:, g:g + 1]).then_inc(hi_ok, 1)
                            else:
                                act.activation(dst, src, ACT.Copy).then_inc(hi_ok, 1)
                        elif kind == "pq" and ends(it):
                            _, g, n, _ = it
                            src = full(it[:3])
                            i = q_units.index(it[:3])
                            if i >= 2:
                                act.wait_ge(qs_ok, 2 * (i - 2) + 1)
                            act.activation(sq[:, n], src, ACT.Square, bias=bq[:, g:g + 1]).then_inc(sq_ok, 1)
                            act.activation(qb[:, n], src, ACT.Identity, bias=bq[:, g:g + 1]).then_inc(emptied["act"], 1)
                        elif kind == "ss":
                            _, g, n = it
                            i = q_units.index(("pq", g, n))
                            if i >= 2:
                                act.wait_ge(qlo_ok, i - 1)
                            link(act.activation(qy[:, n], full(it), ACT.Ln))
                            link(act.activation(qy[:, n], qy[:, n], ACT.Exp, scale=-0.5))
                            act.activation(sq[:, n], qy[:, n], ACT.Square).then_inc(y_ok, 1)
                        elif kind == "s3":
                            _, g, n = it
                            i = q_units.index(("pq", g, n))
                            act.wait_ge(qn_ok, i + 1)
                            act.activation(qy[:, n], qb[:, n], ACT.Identity, scale=tau[:, g:g + 1], bias=et[:, g:g + 1]).then_inc(qs_ok, 1)
                            act.wait_ge(qs_ok, 2 * i + 1)
                            if n == 0:
                                wait_copies_left(act, it)
                            act.activation(cq["hi"][:, n * HALF:(n + 1) * HALF], qy[:, n], ACT.Copy).then_inc(qs_ok, 1)
                        elif kind == "vp" and not ffn:
                            t = it[1]
                            src = full(it)
                            act.activation(v[:, :, t * P:(t + 1) * P], src.rearrange("p (g c) -> p g c", g=NG), ACT.Copy).then_inc(emptied["act"], 1)
                        elif kind == "S":
                            _, T, e = it
                            u = T * G + e
                            dst, prior = exp_buffer(T, e)
                            h = T // TT
                            act.wait_ge(scored, u + 1)
                            if prior:
                                s, head = prior
                                act.wait_ge(weighed, s + 1)
                                act.wait_ge(added_ok[ph.ADDER[head]], adds(s, head))
                            if T % TT == 0 and h >= 2 and e == 0:
                                wait_full(act, ("sm", h // 2 - 1, h % 2))
                            act.activation(dst, scores[:, u % 3, :], ACT.Exp, scale=ph.SCALE).then_inc(probs_ok, 1)
                        elif kind == "sm":
                            _, g, n = it
                            h = 2 * g + n
                            src = full(it)
                            if h:
                                act.wait_ge(out_ok, h)
                            link(act.activation(rn[:], src, ACT.Ln))
                            act.activation(rn[:], rn[:], ACT.Exp, scale=-1.0).then_inc(rinv_ok, 1)
                        elif kind == "hs":
                            t = it[1]
                            act.wait_ge(out_ok, HALVES - 1 if t < TT // 2 else HALVES)
                            if t == 0:
                                wait_copies_left(act, it)
                            elif t >= 4:
                                wait_full(act, ("op", t - 4))
                            act.activation(split_slot(t)[0], outputs(t), ACT.Copy).then_inc(h_hi_ok, 1)
                        elif kind == "gm":
                            act.wait_ge(gates_in, 1)
                            act.activation(eg[:], lg[:], ACT.Exp).then_inc(gates_exp, 1)

                @block.vector
                def _(dve):
                    chain = [0]

                    def link(ins):
                        chain[0] += 1
                        ins.then_inc(dve_chain, 1)
                        dve.wait_ge(dve_chain, chain[0])

                    def full(unit):
                        wait_full(dve, unit)
                        return aux[:, o.bank[unit], :]

                    def newton(y, x, y2, out):
                        link(dve.scalar_tensor_tensor(y2, y2, -0.5, x, ALU.mult, ALU.mult))
                        return dve.scalar_tensor_tensor(out, y2, 1.5, y, ALU.add, ALU.mult)

                    for it in sched:
                        kind = it[0]
                        if kind in ("ln", "l2"):
                            n = it[1]
                            tiles = range(TT // 2)
                            r = slice(n * TT // 2, (n + 1) * TT // 2)
                            if kind == "ln":
                                dve.wait_ge(xs_loaded[2 + n], 16)
                                for t in tiles:
                                    ins = dve.bn_stats(st[:, r.start + t, :], xs[:, t, :])
                                link(ins)
                                for t in tiles:
                                    ins = dve.bn_aggr(mv[:, r.start + t, :], st[:, r.start + t, :])
                                link(ins)
                                dve.tensor_scalar(rs[:, 0, r], mv[:, r, 1], EPS, None, ALU.add).then_inc(rstd_in, 1)
                                continue
                            dve.wait_ge(rstd_in, n + 1)
                            dve.wait_ge(rstd_ok, n + 1)
                            link(dve.tensor_tensor(rs[:, 2, r], rs[:, 1, r], rs[:, 1, r], ALU.mult))
                            link(newton(rs[:, 1, r], rs[:, 0, r], rs[:, 2, r], rs[:, 1, r]))
                            dve.scalar_tensor_tensor(rs[:, 0, r], mv[:, r, 0], -1.0, rs[:, 1, r], ALU.mult, ALU.mult).then_inc(norm_in, 1)
                        elif kind == "trl":
                            _, n, k = it
                            unit = ("tr", n, k)
                            src = full(unit)
                            q = slice(n * HALF, (n + 1) * HALF)
                            dve.wait_ge(hi_ok, hi_units.index(unit) + 1)
                            dve.tensor_tensor(xT_lo[:, k, q], src, xT_hi[:, k, q].bitcast(F32), ALU.subtract).then_inc(emptied["dve"], 1)
                        elif kind in ("pkl", "pql"):
                            _, g, n = it
                            unit = (kind[:2], g, n)
                            src = full(unit)
                            q = slice(n * HALF, (n + 1) * HALF)
                            c = cq if kind == "pql" else ck
                            dve.wait_ge(hi_ok, hi_units.index(unit) + 1)
                            if ffn:
                                ins = dve.scalar_tensor_tensor(c["lo"][:, q], src, bk[:, g:g + 1], c["hi"][:, q].bitcast(F32), ALU.add, ALU.subtract)
                            else:
                                ins = dve.tensor_tensor(c["lo"][:, q], src, c["hi"][:, q].bitcast(F32), ALU.subtract)
                            ins.then_inc(emptied["dve"], 1)
                        elif kind == "s2":
                            _, g, n = it
                            unit = ("ss", g, n)
                            i = q_units.index(("pq", g, n))
                            src = full(unit)
                            dve.wait_ge(y_ok, i + 1)
                            wait_emptied(dve, ("pq", g, n))
                            dve.scalar_tensor_tensor(sq[:, n], sq[:, n], -0.5, src, ALU.mult, ALU.mult).then_inc(emptied["dve"], 1)
                            wait_emptied(dve, unit)
                            link(dve.scalar_tensor_tensor(qy[:, n], sq[:, n], 1.5, qy[:, n], ALU.add, ALU.mult))
                            dve.tensor_tensor(qb[:, n], qb[:, n], qy[:, n], ALU.mult).then_inc(qn_ok, 1)
                        elif kind == "vp" and ffn:
                            t = it[1]
                            src = full(it)
                            dve.tensor_tensor(v[:, :, t * P:(t + 1) * P], src.rearrange("p (g c) -> p g c", g=NG),
                                              bv[:].rearrange("p (g c) -> p g c", g=NG), ALU.add).then_inc(emptied["dve"], 1)
                        elif kind == "mx":
                            _, g, e, t, j = it
                            src = full(it)
                            dve.tensor_reduce(mx[:, e * TT + t, j:j + 1], src, axis=AX.X, op=ALU.max).then_inc(emptied["dve"], 1)
                        elif kind == "nm":
                            g = it[1]
                            wait_emptied(dve, ("mx", g, G - 1, TT - 1, 1))
                            dve.tensor_reduce(nm[:], mx[:], axis=AX.X, op=ALU.max, negate=True).then_inc(nm_ok, 1)
                        elif kind == "ml":
                            g = it[1]
                            src = full(("mt", g))
                            before = [x[1] for x in sched[:o.pos[it]] if x[0] == "md"]
                            if before:
                                dve.wait_ge(m_stacked[before[-1] % 2], G * 16 * o.nth(("md", before[-1]), it, mine(before[-1])))
                            dve.tensor_copy(mrow[:], src[0:G * TT, 0:P]).then_inc(emptied["dve"], 1)
                        elif kind == "ad" and it[1] % TT and it[1] <= LAST_ADDED:
                            add(dve, "dve", it[1])
                        elif kind == "hs":
                            t = it[1]
                            hi, lo = split_slot(t)
                            dve.wait_ge(h_hi_ok, t + 1)
                            dve.tensor_tensor(lo, outputs(t), hi.bitcast(F32), ALU.subtract).then_inc(h_lo_ok, 1)
                        elif kind == "ev":
                            _, g, n = it
                            h = 2 * g + n
                            src = full(("sm", g, n))
                            dve.wait_ge(rinv_ok, h + 1)
                            dve.scalar_tensor_tensor(vh[:, h, :], src, -1.0, rn[:], ALU.mult, ALU.mult).then_inc(emptied["dve"], 1)
                            wait_emptied(dve, ("sm", g, n))
                            link(dve.scalar_tensor_tensor(rn[:], vh[:, h, :], 2.0, rn[:], ALU.add, ALU.mult))
                            dve.tensor_tensor(vh[:, h, :], acc[:, h % 2, :], rn[:], ALU.mult).then_inc(out_ok, 1)
                        elif kind == "gm":
                            src = full(("gt",))
                            for t in range(TT):
                                ins = dve.tensor_tensor(lg[:, t, :], src[:, t * GC:(t + 1) * GC], bg[:], ALU.add)
                            ins.then_inc(emptied["dve"], 1)
                            wait_emptied(dve, ("gt",))
                            dve.tensor_reduce(gm[:, :, 0], lg[:, :, 0:NE], axis=AX.X, op=ALU.max)
                            link(dve.tensor_reduce(gm[:, :, 1], lg[:, :, SH:SH + 2], axis=AX.X, op=ALU.max))
                            dve.tensor_tensor(lg[:, :, 0:NE], lg[:, :, 0:NE], gm[:, :, 0:1].to_broadcast([P, TT, NE]), ALU.subtract)
                            dve.tensor_tensor(lg[:, :, SH:SH + 2], lg[:, :, SH:SH + 2], gm[:, :, 1:2].to_broadcast([P, TT, 2]), ALU.subtract).then_inc(gates_in, 1)
                            dve.wait_ge(gates_exp, 1)
                            for t in range(TT):
                                dve.max(top[:, t, :], eg[:, t, 0:NE])
                            dve.tensor_reduce(g1[:, 0], eg[:, :, 0:NE], axis=AX.X, op=ALU.add)
                            link(dve.tensor_reduce(g1[:, 1], eg[:, :, SH:SH + 2], axis=AX.X, op=ALU.add))
                            link(dve.tensor_reduce(g1[:, 2], top[:, :, 0:TOPK], axis=AX.X, op=ALU.add))
                            link(dve.reciprocal(g1[:, 0:2], g1[:, 0:2]))
                            dve.tensor_tensor(g1[:, 2], g1[:, 2], g1[:, 0], ALU.mult)
                            dve.tensor_tensor(sw[:, :, 0], eg[:, :, SH], g1[:, 1], ALU.mult)
                            link(dve.tensor_tensor(sw[:, :, 1], eg[:, :, SH + 1], g1[:, 1], ALU.mult))
                            link(dve.tensor_tensor(g1[:, 3], sw[:, :, 0], sw[:, :, 1], ALU.add))
                            dve.scalar_tensor_tensor(g1[:, 0], g1[:, 3], 2.0, sw[:, :, 0], ALU.mult, ALU.mult)
                            link(dve.scalar_tensor_tensor(g1[:, 1], g1[:, 2], 2.0 * TOPK, sw[:, :, 1], ALU.mult, ALU.mult))
                            link(dve.tensor_tensor(g1[:, 0], g1[:, 0], g1[:, 1], ALU.add))
                            link(dve.tensor_scalar(sc[:], g1[:, 0], tg[:, 0:1], None, ALU.mult))
                        elif kind == "op":
                            t = it[1]
                            src = full(it)
                            dve.wait_ge(biased, t + 1)
                            by = sc[:, t:t + 1] if ffn else tg[:, 0:1]
                            x = xs[:, t % (TT // 2), :]
                            dve.scalar_tensor_tensor(x, src, by, x, ALU.mult, ALU.add).then_inc(emptied["dve"], 1)

            for i, s in enumerate(made):
                (nc.sync, nc.scalar, nc.vector, nc.gpsimd)[i % 4].sem_clear(s)
            nc.all_engine_barrier()

        one = lambda a, i: None if a is None else a[i:i + 1]
        turn(schedule(ph, False, True), None, None, one(x_in, 0), one(ctxT, 0))
        x_later, ctx_later = x_in[1:B], None if ctxT is None else ctxT[1:B]
        with nc.Fori(0, B - 1) as b:
            at = bass.ds(b, 1)
            turn(schedule(ph, True, True), x_in[at], x_out[at], x_later[at], None if ctxT is None else ctx_later[at])
        turn(schedule(ph, True, False), x_in[B - 1:B], x_out[B - 1:B], None, None)
        for s in (c_in, c_ms, c_act, c_dve, c_abs, c_pool):
            nc.sync.sem_clear(s)
        nc.all_engine_barrier()


def build(nc, x, ctxT, weights, g_xattn, g_ffn, xattn_bo, bq, bk, bv, bp, wg, bg, temp, emb, out):
    w_split = nc.dram_tensor("w_split", [8, 2, NG, P, NG, P], F32).ap()
    x1 = nc.dram_tensor("x_after_xattn", [B, N, DM], F32).ap()
    split_weights(nc, weights, w_split)
    attention_phase(nc, Phase(False), x, ctxT, w_split, xattn_bo, g_xattn, x1, {})
    attention_phase(nc, Phase(True), x1, None, w_split, bp, g_ffn, out,
                    dict(bq=bq, bk=bk, bv=bv, wg=wg, bg=bg, temp=temp, emb=emb))


def kernel(**inputs):
    import numpy as np
    import concourse.bacc as bacc
    from concourse.bass_utils import run_bass_kernel_spmd

    a = {k: np.asarray(v) for k, v in inputs.items()}
    pad = lambda w: np.concatenate([w, np.zeros((DM - w.shape[0], DM), w.dtype)]) if w.shape[0] < DM else w
    channels = lambda v: np.ascontiguousarray(v.reshape(NG, P).T)
    zero = np.zeros(1, np.float32)
    arrays = {
        "x": a["x"],
        "ctxT": np.ascontiguousarray(a["ctx_768"].transpose(0, 2, 1)),
        "weights": np.stack([a["L0_xattn_Wq"], pad(a["L0_xattn_Wk"]), pad(a["L0_xattn_Wv"]), a["L0_xattn_Wo"],
                             a["L0_ffn_Wq"].T, a["L0_ffn_Wk"].T, a["L0_ffn_Wv"].T, a["L0_ffn_Wp"].T]),
        "g_xattn": a["g_xattn"], "g_ffn": a["g_ffn"], "xattn_bo": a["L0_xattn_bo"],
        "bq": channels(a["L0_ffn_bq"]), "bk": channels(a["L0_ffn_bk"]), "bv": a["L0_ffn_bv"], "bp": a["L0_ffn_bp"],
        "wg": np.concatenate([a["L0_ffn_Wr"].T, np.zeros((DM, 1), np.float32), a["L0_ffn_Ws"].T], axis=1),
        "bg": np.concatenate([a["L0_ffn_br"], zero, a["L0_ffn_bs"]]),
        "temp": np.ascontiguousarray(a["L0_ffn_temperature"].reshape(NG, NG).T),
        "emb": channels(a["L0_ffn_query_embedding"].reshape(-1)),
    }
    nc = bacc.Bacc("TRN2", target_bir_lowering=False, num_devices=1, dynamic_dma_scratch_size=1024)
    feed, args = {}, []
    for name, arr in arrays.items():
        arr = np.ascontiguousarray(arr)
        feed[f"in_{name}"] = arr
        args.append(nc.dram_tensor(f"in_{name}", arr.shape, mybir.dt.from_np(arr.dtype), kind="ExternalInput").ap())
    out = nc.dram_tensor("out", [B, N, DM], F32, kind="ExternalOutput").ap()
    build(nc, *args, out)
    return run_bass_kernel_spmd(nc, [feed], core_ids=[0]).results[0]["out"]
```
